# Optimizing a Trainium2 kernel written in Bass

```python
import numpy as np
import jax
import jax.numpy as jnp

def _softmax(x, axis=-1):
    return jax.nn.softmax(x, axis=axis)

def _gelu(x):
    return jax.nn.gelu(x, approximate=True)

def _silu(x):
    return jax.nn.silu(x)

def _sigmoid(x):
    return jax.nn.sigmoid(x)

def _layernorm(x, axis=-1, eps=1e-05):
    m = jnp.mean(x, axis=axis, keepdims=True)
    v = jnp.var(x, axis=axis, keepdims=True)
    return (x - m) / jnp.sqrt(v + eps)

def _scatter_add(tgt, idx, src, axis=0):
    return tgt.at[idx].add(src)

def _segment_sum(src, seg, n):
    return jax.ops.segment_sum(src, seg, n)
kernel_name = 'mk_gnn_resnorm_d2_gnn_r8_8b49ae'

def setup_inputs(seed: int=0):
    np.random.seed(seed)
    _w = jnp.asarray

    def _rec_inputs():
        import jax
        import jax.numpy as jnp
        _gk = jax.random.key(seed)
        x = -0.000202 + 1 * jax.random.normal(jax.random.fold_in(_gk, 1), (12500, 64), jnp.float32)
        src = jax.random.randint(jax.random.fold_in(_gk, 2), (400000,), 0, 12500, jnp.int32)
        dst = jnp.minimum((12500 * jax.random.uniform(jax.random.fold_in(_gk, 3), (400000,)) ** 2.0).astype(jnp.int32), 99999)
        _o = jnp.argsort(dst, stable=True)
        src = src[_o]
        dst = dst[_o]
        edge_attr_32 = -8.62073e-06 + 0.999901 * jax.random.normal(jax.random.fold_in(_gk, 11), (400000, 32), jnp.float32)
        return (x, src, dst, edge_attr_32)
    x, src, dst, edge_attr_32 = _rec_inputs()

    def _L0_gnn_setup():
        import jax, jax.numpy as jnp
        import numpy as np
        N_NODES = 12500
        N_EDGES = 125000
        NODE_DIM = 64
        EDGE_DIM = 32
        EPS = 1e-05
        SLOPE = 0.1

        def _mlp2(v, W1, b1, W2, b2):
            h = jax.nn.leaky_relu(v @ W1 + b1, negative_slope=SLOPE)
            return h @ W2 + b2
        key = jax.random.key(seed)
        ks = jax.random.split(key, 8)
        s = 0.05
        return {'x': jax.random.normal(ks[0], (N_NODES, NODE_DIM), dtype=jnp.float32), 'edge_attr': jax.random.normal(ks[1], (N_EDGES, EDGE_DIM), dtype=jnp.float32), 'W1n': jax.random.normal(ks[2], (NODE_DIM, 2 * NODE_DIM), dtype=jnp.float32) * s, 'b1n': jnp.zeros((2 * NODE_DIM,), dtype=jnp.float32), 'W2n': jax.random.normal(ks[3], (2 * NODE_DIM, NODE_DIM), dtype=jnp.float32) * s, 'b2n': jnp.zeros((NODE_DIM,), dtype=jnp.float32), 'W1e': jax.random.normal(ks[4], (EDGE_DIM, NODE_DIM), dtype=jnp.float32) * s, 'b1e': jnp.zeros((NODE_DIM,), dtype=jnp.float32), 'W2e': jax.random.normal(ks[5], (NODE_DIM, NODE_DIM), dtype=jnp.float32) * s, 'b2e': jnp.zeros((NODE_DIM,), dtype=jnp.float32), 'res_w': jnp.ones((1,), dtype=jnp.float32), 'dp_scale': jnp.ones((1,), dtype=jnp.float32), 'gamma': jnp.ones((NODE_DIM,), dtype=jnp.float32), 'beta': jnp.zeros((NODE_DIM,), dtype=jnp.float32), 'edge_index': jax.random.randint(ks[6], (2, N_EDGES), 0, N_NODES, dtype=jnp.int64) if jax.config.jax_enable_x64 else jax.random.randint(ks[6], (2, N_EDGES), 0, N_NODES, dtype=jnp.int32)}
    _L0_gnn_all = _L0_gnn_setup()
    _L0_gnn_in = {k: v for k, v in _L0_gnn_all.items() if k in ('W1n', 'b1n', 'W2n', 'b2n', 'W1e', 'b1e', 'W2e', 'b2e', 'res_w', 'dp_scale', 'gamma', 'beta')}
    del _L0_gnn_all

    def _L1_gnn_setup():
        import jax, jax.numpy as jnp
        import numpy as np
        N = 8192
        E = 131072
        K = 2
        key = jax.random.key(seed)
        k1, k2, k3, k4 = jax.random.split(key, 4)
        x = jax.random.normal(k1, (N, 64), dtype=jnp.float32)
        edge_index = jax.random.randint(k2, (2, E), 0, N, dtype=jnp.int64)
        W = jax.random.normal(k3, (64, 64), dtype=jnp.float32) * (1.0 / np.sqrt(64))
        b = jax.random.normal(k4, (64,), dtype=jnp.float32) * 0.01
        return {'x': x, 'edge_index': edge_index, 'W': W, 'b': b}
    _L1_gnn_all = _L1_gnn_setup()
    _L1_gnn_in = {k: v for k, v in _L1_gnn_all.items() if k in ('W', 'b')}
    del _L1_gnn_all
    return {'x': x, 'src': src, 'dst': dst, 'edge_attr_32': edge_attr_32, 'L0_gnn_W1n': _L0_gnn_in['W1n'], 'L0_gnn_b1n': _L0_gnn_in['b1n'], 'L0_gnn_W2n': _L0_gnn_in['W2n'], 'L0_gnn_b2n': _L0_gnn_in['b2n'], 'L0_gnn_W1e': _L0_gnn_in['W1e'], 'L0_gnn_b1e': _L0_gnn_in['b1e'], 'L0_gnn_W2e': _L0_gnn_in['W2e'], 'L0_gnn_b2e': _L0_gnn_in['b2e'], 'L0_gnn_res_w': _L0_gnn_in['res_w'], 'L0_gnn_dp_scale': _L0_gnn_in['dp_scale'], 'L0_gnn_gamma': _L0_gnn_in['gamma'], 'L0_gnn_beta': _L0_gnn_in['beta'], 'L1_gnn_W': _L1_gnn_in['W'], 'L1_gnn_b': _L1_gnn_in['b']}

def reference(x, src, dst, edge_attr_32, L0_gnn_W1n, L0_gnn_b1n, L0_gnn_W2n, L0_gnn_b2n, L0_gnn_W1e, L0_gnn_b1e, L0_gnn_W2e, L0_gnn_b2e, L0_gnn_res_w, L0_gnn_dp_scale, L0_gnn_gamma, L0_gnn_beta, L1_gnn_W, L1_gnn_b):
    import jax
    import jax.numpy as jnp

    def _L0_gnn_ref(x, edge_attr, W1n, b1n, W2n, b2n, W1e, b1e, W2e, b2e, res_w, dp_scale, gamma, beta, edge_index):
        import jax, jax.numpy as jnp
        import numpy as np
        N_NODES = 12500
        N_EDGES = 125000
        NODE_DIM = 64
        EDGE_DIM = 32
        EPS = 1e-05
        SLOPE = 0.1

        def _mlp2(v, W1, b1, W2, b2):
            h = jax.nn.leaky_relu(v @ W1 + b1, negative_slope=SLOPE)
            return h @ W2 + b2
        num_nodes = x.shape[0]
        x_t = _mlp2(x, W1n, b1n, W2n, b2n)
        e_t = _mlp2(edge_attr, W1e, b1e, W2e, b2e)
        src, dst = (edge_index[0], edge_index[1])
        msgs = x_t[src] * e_t * dp_scale
        aggregated = jax.ops.segment_sum(msgs, dst, num_segments=num_nodes)
        out = x + aggregated * res_w
        mu = jnp.mean(out, axis=-1, keepdims=True)
        var = jnp.mean(jnp.square(out - mu), axis=-1, keepdims=True)
        return (out - mu) * jax.lax.rsqrt(var + EPS) * gamma + beta

    def _L1_gnn_ref(x, edge_index, W, b):
        import jax, jax.numpy as jnp
        import numpy as np
        N = 8192
        E = 131072
        K = 2
        n = x.shape[0]
        loops = jnp.arange(n, dtype=edge_index.dtype)
        row = jnp.concatenate([edge_index[0], loops])
        col = jnp.concatenate([edge_index[1], loops])
        deg = jax.ops.segment_sum(jnp.ones_like(col, dtype=x.dtype), col, num_segments=n)
        deg_inv_sqrt = jnp.where(deg > 0, jax.lax.rsqrt(jnp.maximum(deg, 1e-12)), 0.0).astype(x.dtype)
        edge_weight = deg_inv_sqrt[row] * deg_inv_sqrt[col]
        h = x
        for _ in range(K):
            msgs = edge_weight[:, None] * h[col]
            h = jax.ops.segment_sum(msgs, row, num_segments=n)
        out = h @ W.T + b
        return out
    edge_index = jnp.stack([src, dst])
    x = _layernorm(x + _L0_gnn_ref(x, edge_attr_32, L0_gnn_W1n, L0_gnn_b1n, L0_gnn_W2n, L0_gnn_b2n, L0_gnn_W1e, L0_gnn_b1e, L0_gnn_W2e, L0_gnn_b2e, L0_gnn_res_w, L0_gnn_dp_scale, L0_gnn_gamma, L0_gnn_beta, edge_index), axis=-1)
    x = _layernorm(x + _L1_gnn_ref(x, edge_index, L1_gnn_W, L1_gnn_b), axis=-1)
    return x

_drawn_inputs = setup_inputs


def setup_inputs(seed=0):
    import zlib

    import numpy as np

    out = dict(_drawn_inputs(seed))
    spreads = {'L0_gnn_b1n': (0.0, 0.1),
     'L0_gnn_b2n': (0.0, 0.1),
     'L0_gnn_b1e': (0.0, 0.1),
     'L0_gnn_b2e': (0.0, 0.1),
     'L0_gnn_gamma': (1.0, 0.2),
     'L0_gnn_beta': (0.0, 0.1)}
    factors = {'L1_gnn_b': 4.86}
    for name, (base, spread) in spreads.items():
        noise = np.random.default_rng([zlib.crc32(name.encode()), seed]).standard_normal(out[name].shape)
        drawn = base * np.exp(spread * noise) if base else spread * noise
        out[name] = jnp.asarray(drawn.astype(out[name].dtype))
    for name, factor in factors.items():
        out[name] = (out[name] * factor).astype(out[name].dtype)
    return out
```

```python
import concourse.bass as bass
from concourse import mybir
from contextlib import ExitStack


def gnn_two_layers(nc, x, src, dst, edge_attr, W1n, b1n, W2n, b2n, W1e, b1e, W2e, b2e,
                   res_w, dp_scale, gamma, beta, W, b, out):
    f32, i32, bf16 = mybir.dt.float32, mybir.dt.int32, mybir.dt.bfloat16
    ALU, ACT, AX = mybir.AluOpType, mybir.ActivationFunctionType, mybir.AxisListType

    P = 128
    N, D = x.shape
    E, DE = edge_attr.shape
    HN = W1n.shape[1]
    EPS = 1e-5
    SLOPE = 0.1
    K = 25
    GE = K * P
    G = E // GE
    assert G * GE == E and HN == P and D == 64 and DE == 32
    B = -(-N // P)
    NL = N - (B - 1) * P
    R = D + 2
    Q = 4
    S = -(-K // Q)
    W_OF = [min(Q, K - Q * s) for s in range(S)]
    BIAS = 2 * S
    BP = B
    NP = B // 2
    assert B % 2 == 0 and NP % 2 == 1
    assert B * Q <= 512

    ctx = ExitStack()
    with ctx:
        def sb(name, shape, dt=f32):
            return ctx.enter_context(nc.sbuf_tensor(name, shape, dt))

        def sem(name):
            return ctx.enter_context(nc.semaphore(name))

        node_rows = nc.dram_tensor("node_rows", [BP * P, D], f32).ap()
        hop_rows = nc.dram_tensor("hop_rows", [BP * P, D], f32).ap()
        sorted_rows = nc.dram_tensor("sorted_rows", [E, R], f32).ap()
        range_dram = nc.dram_tensor("range_dram", [4, P], i32).ap()

        X = sb("X", [P, BP, D])
        TAB_W = max(B * (D + 1), 2 * GE)
        tab = sb("tab", [P, TAB_W])
        agg0 = tab[:, 0:B * (D + 1)].rearrange("p (b f) -> p b f", f=D + 1)
        dst_row = tab[:, 0:2 * GE].bitcast(i32).rearrange("p (q e) -> p q e", q=2)
        U = sb("U", [P, BP, D])
        H = sb("H", [P, BP, D])
        src_i = sb("src_i", [P, G, K], i32)
        dst_i = sb("dst_i", [P, G, K], i32)
        ea = sb("ea", [P, 2, K, DE])
        eaT = sb("eaT", [P, 2, P])
        hb = sb("hb", [P, 2, 2 * P])
        hl = sb("hl", [P, 2, 2 * P])
        rows = sb("rows", [P, 2, K, D])
        msg = sb("msg", [P, 2, K, R])
        OH = sb("OH", [P, K, P])
        ob = sb("ob", [P, 2, Q, B], bf16)
        rank_w = sb("rank_w", [P, Q, B])
        idx = sb("idx", [P, 2, K], i32)
        bucket = sb("bucket", [P, 2, K], i32)
        pos_f = sb("pos_f", [P, 2, K])
        pos_i = sb("pos_i", [P, 2, K], i32)
        iota_n = sb("iota_n", [P, P])
        block0 = sb("block0", [P, BP])
        node_id = sb("node_id", [P, BP])
        ident = sb("ident", [P, P])
        upper = sb("upper", [P, P], bf16)
        upper_f = sb("upper_f", [P, P])
        counts_T = sb("counts_T", [P, P])
        ones_b = sb("ones_b", [P, P], bf16)
        zeros_b = sb("zeros_b", [1, 512], bf16)
        assert (Q + 1) * B <= 512
        ones_f = sb("ones_f", [1, P])
        w1n = sb("w1n", [P, 2, P])
        w2n = sb("w2n", [P, D])
        b1n_c = sb("b1n_c", [P, 1])
        b2n_r = sb("b2n_r", [1, D])
        w1e = sb("w1e", [P, 2, P])
        w2e = sb("w2e", [P, 2, D])
        b1e_c = sb("b1e_c", [P, 1])
        b2e_r = sb("b2e_r", [1, D])
        w_sb = sb("w_sb", [D, 2, D])
        wT = sb("wT", [P, 2, D])
        b_r = sb("b_r", [1, D])
        gam = sb("gam", [P, D])
        bet = sb("bet", [P, D])
        scl = sb("scl", [P, 2])
        scale = sb("scale", [P, 1])
        mean = sb("mean", [P, BP])
        var = sb("var", [P, BP])
        std = sb("std", [P, BP])
        dinv = sb("dinv", [P, BP])
        count_b = sb("count_b", [P, B])
        base_b = sb("base_b", [P, B])
        thr = sb("thr", [P, 2])
        cmp_w = sb("cmp_w", [P, 2, B])
        rng_f = sb("rng_f", [P, 2])
        rng_i = sb("rng_i", [P, 2], i32)
        dst_g = OH[:, :, :].rearrange("p k e -> p (k e)").bitcast(i32)
        rng_d = sb("rng_d", [1, 4, P], i32)

        bank = [ctx.enter_context(nc.psum_tensor(f"bank{i}", [P, 512], f32)) for i in range(8)]

        s_turn = {k: sem(f"{k}_turns") for k in ("sync", "gpsimd", "vector")}
        s_fill = sem("fills_landed")
        s_const = sem("constants_made")
        s_wzero = sem("weight_tiles_zeroed")
        s_load = sem("weights_loaded")
        s_xld = sem("x_loaded")
        s_ids = sem("indices_loaded")
        s_dg = sem("dst_groups_loaded")
        s_dv = sem("vector_op_done")
        s_rngd = sem("ranges_made")
        s_rngst = sem("ranges_stored")
        s_rngld = [sem("dst_ranges_loaded"), sem("src_ranges_loaded")]
        s_xr = [sem(f"x_pair_in{q}") for q in range(2)]
        s_xT = sem("x_transposed")
        s_xTs = sem("x_transpose_copied")
        s_n1 = sem("node_layer1_done")
        s_nb = sem("node_bias_done")
        s_nl = sem("node_leaky_done")
        s_n2 = sem("node_layer2_done")
        s_nc = sem("node_rows_copied")
        s_nst = sem("node_rows_stored")
        s_ea = [sem(f"edge_features_in{q}") for q in range(2)]
        s_idx = [sem(f"src_indices_in{q}") for q in range(2)]
        s_ix6 = sem("dst_indices_copied")
        s_tp = sem("edge_transposed")
        s_tc = sem("edge_transpose_copied")
        s_l1 = sem("edge_layer1_done")
        s_eb = sem("edge_bias_done")
        s_lk = sem("edge_leaky_done")
        s_l2 = sem("edge_layer2_done")
        s_msg = sem("messages_made")
        s_bk = sem("bucket_ids_made")
        s_ob = sem("buckets_marked")
        s_hist = sem("buckets_counted")
        s_total = sem("bucket_totals_ready")
        s_rows = [[sem(f"rows_gathered{q}_{s}") for s in range(S)] for q in range(2)]
        s_var = sem("variance_made")
        s_dev = sem("deviation_made")
        s_cT = sem("counts_transposed")
        s_cTs = sem("counts_transpose_copied")
        s_bases = sem("bases_summed")
        s_g1 = sem("stage3_done")
        s_row = [sem(f"dst_row_in{q}") for q in range(2)]
        s_m4 = [sem(f"node_marks{i}") for i in range(S)]
        s_u4 = [sem(f"node_marks_used{i}") for i in range(S)]
        s_sel = sem("group_rows_selected")
        s_rec = sem("group_rows_copied")
        s_bk4 = sem("bucket_ids_made_again")
        s_ob4 = sem("buckets_marked_again")
        s_pa = sem("ranks_ready")
        s_pl = sem("places_of_blocks_added")
        s_run = sem("next_places_advanced")
        s_pm = sem("ranks_picked")
        s_pr = sem("positions_summed")
        s_pi = sem("positions_rounded")
        s_sc = [sem(f"rows_scattered{q}") for q in range(2)]
        s_m = [sem(f"sorted_rows_in{q}") for q in range(2)]
        s_srt = sem("sorted_ids_kept")
        s_free5 = sem("stage5_group_summed")
        s_g2 = sem("hop_rows_made")
        s_g2st = sem("hop_rows_stored")
        s_rows6 = [sem(f"hop_rows_gathered{q}") for q in range(2)]
        s_free6 = sem("stage6_group_summed")
        s_wT = sem("W_transposed")
        s_wTs = sem("W_transpose_copied")
        s_ha = sem("hop_sum_with_loop")
        s_h2 = sem("h2_made")
        s_hT = sem("h2_transposed")
        s_hTs = sem("h2_transpose_copied")
        s_lin = sem("last_product_done")
        s_res = sem("residual_added")
        s_fin = sem("output_made")
        s_out = sem("output_stored")

        class Visits:

            def __init__(self, tag):
                self.marks = [sem(f"{tag}_marks{s}") for s in range(S)]
                self.summed = [sem(f"{tag}_summed{s}") for s in range(S)]
                self.added = sem(f"{tag}_added")

        v2, v5, v6 = Visits("dst"), Visits("src1"), Visits("src2")

        block = ctx.enter_context(nc.Block())

        def step(g, s):
            return g * S + s

        def through(n):
            return n + (1 + BIAS)

        def before(g, s):
            return step(g, s) - (1 if s == 0 else 2)

        def tiles(s):
            return slice(Q * s, Q * s + W_OF[s])

        def over(e, count, body, apart=0):
            for i in range(apart):
                body(i, 2 * i, 0)
                body(i, 2 * i + 1, 1)
            with e.Fori(apart, count // 2) as i:
                body(i, i * 2, 0)
                body(i, i * 2 + 1, 1)
            if count % 2:
                body(count // 2, count - 1, 0)

        def over_groups(e, body, apart=0):
            over(e, G, body, apart)

        def pair_through(j):
            return j + 3

        def block_range(e, g, which):
            lo = e.value_load(rng_d[0:1, which, bass.ds(g, 1)], min_val=0, max_val=B - 1)
            hi = e.value_load(rng_d[0:1, which + 1, bass.ds(g, 1)], min_val=0, max_val=B - 1)
            return lo, hi

        N_LOADS = 21
        src_flat = src_i[:, :, :].rearrange("p g k -> p (g k)")
        dst_flat = dst_i[:, :, :].rearrange("p g k -> p (g k)")
        H_flat = H[:, :, :].rearrange("p b f -> p (b f)")

        def src_cols(g):
            return src_flat[:, bass.ds(g * K, K)]

        def dst_cols(g):
            return dst_flat[:, bass.ds(g * K, K)]

        def mark_and_add(e, v, seen, g, which, ids, table, width):
            lo, hi = block_range(e, g, which)
            with e.Fori(lo, hi + 1) as blk:
                n = e.snap(seen)
                for s in range(S):
                    w = W_OF[s]
                    e.wait_ge(v.summed[s], n + 1)
                    nc.vector.scalar_tensor_tensor(
                        out=OH[:, tiles(s), :],
                        in0=ids[:, bass.ds(g * K + Q * s, w)].unsqueeze(2).to_broadcast([P, w, P]),
                        scalar=block0[:, bass.ds(blk, 1)],
                        in1=iota_n[:, :].unsqueeze(1).to_broadcast([P, w, P]),
                        op0=ALU.subtract, op1=ALU.is_equal).then_inc(v.marks[s], 1)
                e.wait_ge(v.summed[S - 1], n + 2)
                e.wait_ge(v.added, n + 1)
                part = table[:, bass.ds(blk * width, width)]
                nc.vector.tensor_tensor(part, part, bank[5][:, 0:width], ALU.add).then_inc(v.added, 1)
                e.reg_add(seen, seen, 1)

        def sum_by_node(e, v, seen, g, which, data):
            lo, hi = block_range(e, g, which)
            width = data.shape[2]
            with e.Fori(lo, hi + 1) as blk:
                n = e.snap(seen)
                e.wait_ge(v.added, n + 1)
                for s in range(S):
                    e.wait_ge(v.marks[s], n + 1)
                    for k in range(Q * s, Q * s + W_OF[s]):
                        mm = nc.tensor.matmul(bank[5][:, 0:width], OH[:, k, :], data[:, k, :],
                                              start=(k == 0), stop=(k == K - 1))
                    mm.then_inc(v.summed[s], 1)
                e.reg_add(seen, seen, 1)

        def row_of(v, n):
            return v.rearrange("(a n) -> a n", a=1) if n is None else \
                v.rearrange("(a n) -> a n", a=1).to_broadcast([n, v.shape[0]])

        @block.sync
        def _(e):
            e.dma_start(dst_g[0:G, :], dst.rearrange("(g e) -> g e", e=GE)).then_inc(s_dg, 16)
            e.wait_ge(s_wzero, 1)
            e.dma_start(X[:, 0:B - 1, :],
                        x[0:(B - 1) * P, :].rearrange("(b p) f -> p b f", p=P)).then_inc(s_xld, 16)
            e.dma_start(X[0:NL, B - 1, :], x[(B - 1) * P:N, :]).then_inc(s_xld, 16)
            for i_sb, i_dr in ((src_i, src), (dst_i, dst)):
                e.dma_start(i_sb[:, :, :], i_dr.rearrange("(g p k) -> p g k", p=P, k=K)).then_inc(s_ids, 16)

            def spread_ranges(n):
                e.wait_ge(s_rngd, n + 1)
                e.dma_start(range_dram[2 * n:2 * n + 2, 0:G].rearrange("a g -> g a"), rng_i[0:G, :],
                            allow_slow_non_contiguous=True).then_inc(s_rngst, 16)
                e.wait_ge(s_rngst, 16 * (n + 1))
                e.dma_start(rng_d[0:1, 2 * n:2 * n + 2, 0:G],
                            range_dram[2 * n:2 * n + 2, 0:G].unsqueeze(0)).then_inc(s_rngld[n], 16)
            spread_ranges(0)

            def load_pair(i, j, q):
                e.wait_ge(s_xT, pair_through(j - 2))
                slot = ea[:, q, 0:4, :].rearrange("p k f -> p (k f)").rearrange("p (b f) -> p b f", b=2)
                if isinstance(j, int) and j == NP - 1:
                    e.dma_start(slot[:, 0, :], x[(B - 2) * P:(B - 1) * P, :]).then_inc(s_xr[q], 16)
                    e.dma_start(slot[0:NL, 1, :], x[(B - 1) * P:N, :]).then_inc(s_xr[q], 16)
                else:
                    e.dma_start(slot, x[bass.ds(j * (2 * P), 2 * P), :]
                                .rearrange("(b p) f -> p b f", p=P)).then_inc(s_xr[q], 16)
            over(e, NP, load_pair)

            e.wait_ge(s_nc, pair_through(NP - 1))
            e.dma_start(node_rows.rearrange("(b p) f -> p b f", p=P), U[:, :, :]).then_inc(s_nst, 16)

            def load_features(i, g, q):
                first = e.snap(g * GE)
                e.wait_ge(s_tp, through(step(g - 2, S - 1)))
                e.dma_start(ea[:, q, :, :],
                            edge_attr[bass.ds(first, GE), :].rearrange("(p k) f -> p k f", k=K))\
                    .then_inc(s_ea[q], 16)
                e.wait_ge(s_msg, through(step(g - 2, S - 1)))
                e.sem_inc(s_turn["sync"], 1)
                e.dma_start(idx[:, q, :], src[bass.ds(first, GE)].rearrange("(p k) -> p k", k=K))\
                    .then_inc(s_idx[q], 16)
            over_groups(e, load_features)

            spread_ranges(1)

            e.wait_ge(s_g1, 1)
            def load_dst_row(i, g, q):
                first = e.snap(g * GE)
                e.wait_ge(s_pi, g + 1)
                e.dma_start(dst_row[:, q, :], dst[bass.ds(first, GE)]
                            .rearrange("(a e) -> a e", a=1).to_broadcast([P, GE])).then_inc(s_row[q], 16)
            over_groups(e, load_dst_row)

            for q in range(2):
                e.wait_ge(s_sc[q], 16 * K * ((G + 1 - q) // 2))
            def load_sorted(i, g, q):
                first = e.snap(g * GE)
                e.wait_ge(s_free5, g + 1)
                e.dma_start(msg[:, q, :, :],
                            sorted_rows[bass.ds(first, GE), :].rearrange("(p k) f -> p k f", k=K))\
                    .then_inc(s_m[q], 16)
            over_groups(e, load_sorted)
            e.wait_ge(s_g2, 1)
            e.dma_start(hop_rows.rearrange("(b p) f -> p b f", p=P), U[:, :, :]).then_inc(s_g2st, 16)

            e.wait_ge(s_fin, 1)
            e.dma_start(out[0:(B - 1) * P, :].rearrange("(b p) f -> p b f", p=P), H[:, 0:B - 1, :])\
                .then_inc(s_out, 16)
            e.dma_start(out[(B - 1) * P:N, :], H[0:NL, B - 1, :]).then_inc(s_out, 16)
            e.wait_ge(s_out, 32)

        @block.gpsimd
        def _(e):
            e.memset(ident[:, :], 0.0).then_inc(s_fill, 1)
            e.memset(upper_f[:, :], 1.0).then_inc(s_fill, 1)
            e.memset(ones_b[:, :], 1.0).then_inc(s_fill, 1)
            e.memset(zeros_b[:, :], 0.0)
            e.memset(ones_f[:, :], 1.0)
            for q in range(2):
                e.memset(msg[:, q, :, :], 1.0)
            small = dict(channel_multiplier=0, allow_small_or_imprecise_dtypes=True)
            e.iota(iota_n[:, :], [[1, P]], base=0, **small)
            e.iota(block0[:, :], [[P, B]], base=0, **small)
            lanes = dict(allow_small_or_imprecise_dtypes=True)
            e.iota(node_id[:, :], [[P, B]], base=0, channel_multiplier=1, **lanes)
            e.iota(thr[:, 0:1], [[0, 1]], base=0, channel_multiplier=GE, **lanes)
            e.iota(thr[:, 1:2], [[0, 1]], base=GE - 1, channel_multiplier=GE, **lanes)
            e.wait_ge(s_fill, 3)
            e.affine_select(out=ident[:, :], in_=ident[:, :], compare_op=ALU.not_equal, fill=1.0,
                            base=0, pattern=[[-1, P]], channel_multiplier=1)
            e.affine_select(out=upper[:, :], in_=ones_b[:, :], compare_op=ALU.is_gt, fill=0.0,
                            base=0, pattern=[[1, P]], channel_multiplier=-1)
            e.affine_select(out=upper_f[:, :], in_=upper_f[:, :], compare_op=ALU.is_gt, fill=0.0,
                            base=0, pattern=[[1, P]], channel_multiplier=-1).then_inc(s_const, 1)

            e.wait_ge(s_ids, 32)
            def gather_nodes(i, g, q):
                e.wait_ge(s_msg, through(step(g - 2, S - 1)))
                e.wait_ge(s_idx[q], (i + 1) * 16)
                e.wait_ge(s_nst, 16)
                e.sem_inc(s_turn["gpsimd"], 1)
                for k in range(K):
                    e.indirect_dma_start(
                        out=rows[:, q, k, :], out_offset=None, in_=node_rows,
                        in_offset=bass.IndirectOffsetOnAxis(ap=idx[:, q, k:k + 1], axis=0),
                    ).then_inc(s_rows[q][k // Q], 16)
            over_groups(e, gather_nodes)

            def scatter_rows(i, g, q):
                e.wait_ge(s_rec, g + 2)
                e.wait_ge(s_pi, g + 3)
                e.sem_inc(s_turn["gpsimd"], 1)
                for k in range(K):
                    e.indirect_dma_start(
                        out=sorted_rows,
                        out_offset=bass.IndirectOffsetOnAxis(ap=pos_i[:, q, k:k + 1], axis=0),
                        in_=msg[:, q, k, :], in_offset=None).then_inc(s_sc[q], 16)
            over_groups(e, scatter_rows)

            def gather_hop(i, g, q):
                e.wait_ge(s_free6, g + 1)
                e.wait_ge(s_ix6, g + 1)
                e.wait_ge(s_g2st, 16)
                e.sem_inc(s_turn["gpsimd"], 1)
                for k in range(K):
                    e.indirect_dma_start(
                        out=rows[:, q, k, :], out_offset=None, in_=hop_rows,
                        in_offset=bass.IndirectOffsetOnAxis(ap=idx[:, q, k:k + 1], axis=0),
                    ).then_inc(s_rows6[q], 16)
            over_groups(e, gather_hop)

        @block.scalar
        def _(e):
            e.wait_ge(s_wzero, 1)
            loads = [(w1n[0:D, 0, :], W1n), (w1n[D:P, 1, :], W1n), (w2n[:, :], W2n),
                     (b1n_c[:, :], b1n.rearrange("(n a) -> n a", a=1)), (b2n_r[:, :], row_of(b2n, None)),
                     (w2e[0:D, 0, :], W2e), (w2e[D:P, 1, :], W2e), (b2e_r[:, :], row_of(b2e, None)),
                     (b1e_c[0:D, :], b1e.rearrange("(n a) -> n a", a=1)),
                     (b1e_c[D:P, :], b1e.rearrange("(n a) -> n a", a=1)),
                     (w_sb[:, 0, :], W), (w_sb[:, 1, :], W), (b_r[:, :], row_of(b, None)),
                     (gam[:, :], row_of(gamma, P)), (bet[:, :], row_of(beta, P)),
                     (scl[:, 0:1], row_of(dp_scale, P)), (scl[:, 1:2], row_of(res_w, P))]
            for t in range(Q):
                loads.append((w1e[DE * t:DE * (t + 1), t // 2, D * (t % 2):D * (t % 2) + D], W1e))
            assert len(loads) == N_LOADS
            for to, of in loads:
                e.dma_start(to, of).then_inc(s_load, 16)

            e.sem_inc(s_xTs, 2)
            e.sem_inc(s_nb, 2)
            e.wait_ge(s_load, 16 * N_LOADS)
            def node_copies(i, j, q):
                e.wait_ge(s_xT, pair_through(j))
                e.wait_ge(s_n1, pair_through(j - 2))
                nc.scalar.activation(eaT[:, q, :], bank[0][:, q * P:(q + 1) * P],
                                     ACT.Copy).then_inc(s_xTs, 1)
                e.wait_ge(s_n1, pair_through(j))
                e.wait_ge(s_nl, pair_through(j - 2))
                nc.scalar.activation(hb[:, q, :], bank[1 + q][:, 0:2 * P], ACT.Identity,
                                     bias=b1n_c[:, :]).then_inc(s_nb, 1)
            over(e, NP, node_copies)

            e.sem_inc(s_tc, BIAS)
            e.sem_inc(s_eb, BIAS)
            def edge_copies(i, g, q):
                def copy_transpose(s):
                    w = W_OF[s] * DE
                    e.wait_ge(s_tp, through(step(g, s)))
                    e.wait_ge(s_l1, through(before(g, s)))
                    nc.scalar.activation(eaT[0:w, s % 2, :], bank[0][0:w, (s % 2) * P:(s % 2 + 1) * P],
                                         ACT.Copy).then_inc(s_tc, 1)

                copy_transpose(0)
                for s in range(S):
                    if s + 1 < S:
                        copy_transpose(s + 1)
                    parts, cols = (P, 2 * P) if W_OF[s] == Q else (D, P)
                    e.wait_ge(s_l1, through(step(g, s)))
                    e.wait_ge(s_lk, through(before(g, s)))
                    nc.scalar.activation(hb[0:parts, s % 2, 0:cols], bank[1 + s % 2][0:parts, 0:cols],
                                         ACT.Identity, bias=b1e_c[0:parts, :]).then_inc(s_eb, 1)
            over_groups(e, edge_copies)

            def deviation(n):
                e.wait_ge(s_var, n + 1)
                nc.scalar.activation(std[:, :], var[:, :], ACT.Sqrt).then_inc(s_dev, 1)
            for n in range(3):
                deviation(n)

            e.sem_inc(s_rec, 1)
            def rows_out(i, g, q):
                if not isinstance(i, int) or i > 0:
                    e.wait_ge(s_sc[q], i * (16 * K))
                nc.scalar.activation(msg[:, q, :, D:D + 1].bitcast(i32), src_cols(g).unsqueeze(2), ACT.Copy)
                nc.scalar.activation(msg[:, q, :, D + 1:R].bitcast(i32), dst_cols(g).unsqueeze(2), ACT.Copy)
                e.wait_ge(s_sel, g + 1)
                for c in range(4):
                    w = min(8, K - 8 * c)
                    last = nc.scalar.activation(
                        msg[:, q, 8 * c:8 * c + w, 0:D],
                        bank[c][:, 0:w * D].rearrange("p (k f) -> p k f", f=D), ACT.Copy)
                last.then_inc(s_rec, 1)
            over_groups(e, rows_out, apart=1)

            def copy_indices(i, g, q):
                e.wait_ge(s_free6, g + 1)
                nc.scalar.activation(idx[:, q, :], dst_cols(g), ACT.Copy).then_inc(s_ix6, 1)
            e.wait_ge(s_srt, G)
            over_groups(e, copy_indices)

            e.wait_ge(s_wT, 1)
            for h in range(2):
                last = nc.scalar.activation(wT[h * D:(h + 1) * D, h, :], bank[3][h * D:(h + 1) * D, 0:D],
                                            ACT.Copy)
            last.then_inc(s_wTs, 1)
            e.sem_inc(s_hTs, 2)
            def h2_copies(i, j, q):
                e.wait_ge(s_hT, pair_through(j))
                e.wait_ge(s_lin, pair_through(j - 2))
                nc.scalar.activation(eaT[:, q, :], bank[0][:, q * P:(q + 1) * P],
                                     ACT.Copy).then_inc(s_hTs, 1)
            over(e, NP, h2_copies)
            deviation(3)

        @block.tensor
        def _(e):
            seen, seen4, seen5, seen6 = (e.alloc_register(f"pe_visits{n}") for n in (2, 4, 5, 6))
            for r in (seen, seen4, seen5, seen6):
                e.reg_mov(r, 0)
            for s_of, n in ((s_xT, 2), (s_n1, 2), (s_n2, 2), (s_tp, BIAS), (s_l1, BIAS), (s_l2, BIAS),
                            (s_hist, BIAS), (s_pa, BIAS), (s_hT, 2), (s_lin, 2)):
                e.sem_inc(s_of, n)
            for v in (v2, v5, v6):
                for s in range(S):
                    e.sem_inc(v.summed[s], 1)
            for s in range(S):
                e.sem_inc(s_u4[s], 1)
            e.wait_ge(s_const, 1)
            e.wait_ge(s_load, 16 * N_LOADS)

            def node_network(i, j, q):
                e.wait_ge(s_xr[q], (i + 1) * 16 if not (isinstance(j, int) and j == NP - 1) else (i + 2) * 16)
                e.wait_ge(s_xTs, pair_through(j - 2))
                nc.tensor.transpose(bank[0][:, q * P:(q + 1) * P],
                                    ea[:, q, 0:4, :].rearrange("p k f -> p (k f)"), ident[:, :])\
                    .then_inc(s_xT, 1)
                e.wait_ge(s_xTs, pair_through(j))
                e.wait_ge(s_nb, pair_through(j - 2))
                for h in range(2):
                    mm = nc.tensor.matmul(bank[1 + q][:, h * P:(h + 1) * P], w1n[:, h, :],
                                          eaT[:, q, :], start=True, stop=True)
                mm.then_inc(s_n1, 1)
                e.wait_ge(s_nl, pair_through(j))
                e.wait_ge(s_nc, pair_through(j - 2))
                for h in range(2):
                    o = bank[3 + q][:, h * D:(h + 1) * D]
                    nc.tensor.matmul(o, ones_f[:, :], b2n_r[:, :], start=True, stop=False)
                    mm = nc.tensor.matmul(o, hl[:, q, h * P:(h + 1) * P], w2n[:, :], start=False, stop=True)
                mm.then_inc(s_n2, 1)
            over(e, NP, node_network)

            e.wait_ge(s_rngld[0], 16)
            nc.tensor.matmul(bank[6][:, 0:B], ones_b[0:1, :], zeros_b[:, 0:B], start=True, stop=False)
            def edge_network(i, g, q):
                def transpose(s):
                    w = W_OF[s] * DE
                    e.wait_ge(s_tc, through(before(g, s)))
                    nc.tensor.transpose(bank[0][0:w, (s % 2) * P:(s % 2 + 1) * P],
                                        ea[:, q, tiles(s), :].rearrange("p k f -> p (k f)"), ident[:, :])\
                        .then_inc(s_tp, 1)

                def layer1(s):
                    e.wait_ge(s_tc, through(step(g, s)))
                    e.wait_ge(s_eb, through(before(g, s)))
                    o = bank[1 + s % 2]
                    if W_OF[s] == Q:
                        for h in range(2):
                            mm = nc.tensor.matmul(o[:, h * P:(h + 1) * P], w1e[:, h, :], eaT[:, s % 2, :],
                                                  start=True, stop=True)
                    else:
                        mm = nc.tensor.matmul(o[0:D, 0:P], w1e[0:DE, 0, 0:D], eaT[0:DE, s % 2, :],
                                              start=True, stop=True)
                    mm.then_inc(s_l1, 1)

                def layer2(s):
                    w = W_OF[s]
                    e.wait_ge(s_lk, through(step(g, s)))
                    e.wait_ge(s_msg, through(before(g, s)))
                    o = bank[3 + s % 2]
                    nc.tensor.matmul(o[:, 0:w * D], ones_f[:, :],
                                     b2e_r[:, :].unsqueeze(1).to_broadcast([1, w, D]), start=True, stop=False)
                    if w == Q:
                        for h in range(2):
                            mm = nc.tensor.matmul(o[:, h * P:(h + 1) * P], hl[:, s % 2, h * P:(h + 1) * P],
                                                  w2e[:, :, :].rearrange("p t f -> p (t f)"),
                                                  start=False, stop=(h == 1))
                    else:
                        mm = nc.tensor.matmul(o[:, 0:D], hl[0:D, s % 2, 0:P], w2e[0:D, 0, :],
                                              start=False, stop=True)
                    mm.then_inc(s_l2, 1)

                e.wait_ge(s_ea[q], (i + 1) * 16)
                transpose(0)
                layer1(0)
                transpose(1)
                for s in range(S):
                    if s + 1 < S:
                        layer1(s + 1)
                    if s + 2 < S:
                        transpose(s + 2)
                    layer2(s)
                    e.wait_ge(s_ob, through(step(g, s)))
                    for k in range(W_OF[s]):
                        mm = nc.tensor.matmul(bank[6][:, 0:B], ones_b[:, :], ob[:, s % 2, k, :],
                                              start=False, stop=False)
                    mm.then_inc(s_hist, 1)
                sum_by_node(e, v2, seen, g, 0, msg[:, q, :, 0:D + 1])
            over_groups(e, edge_network)
            nc.tensor.matmul(bank[6][:, 0:B], ones_b[0:1, :], zeros_b[:, 0:B], start=False, stop=True)\
                .then_inc(s_total, 1)

            e.wait_ge(s_cT, 1)
            nc.tensor.transpose(bank[7][0:B, 0:P], count_b[:, :], ident[:, :]).then_inc(s_cT, 1)
            e.wait_ge(s_cTs, 1)
            nc.tensor.matmul(bank[6][:, 0:B], counts_T[0:B, :], upper_f[0:B, 0:B], start=True, stop=True)\
                .then_inc(s_bases, 1)

            e.wait_ge(s_g1, 1)
            def select_rows(i, g, q):
                e.wait_ge(s_rec, g + 1)
                for c in range(4):
                    nc.tensor.matmul(bank[c][:, :], ones_b[0:1, :], zeros_b[:, :], start=True, stop=False)
                lo, hi = block_range(e, g, 0)
                with e.Fori(lo, hi + 1) as blk:
                    n = e.snap(seen4)
                    for s in range(S):
                        e.wait_ge(s_m4[s], n + 1)
                        for k in range(Q * s, Q * s + W_OF[s]):
                            mm = nc.tensor.matmul(bank[k // 8][:, (k % 8) * D:(k % 8 + 1) * D], OH[:, k, :],
                                                  U[:, bass.ds(blk, 1), :].rearrange("p a f -> p (a f)"),
                                                  start=False, stop=False)
                        mm.then_inc(s_u4[s], 1)
                    e.reg_add(seen4, seen4, 1)
                for c in range(4):
                    mm = nc.tensor.matmul(bank[c][:, :], ones_b[0:1, :], zeros_b[:, :], start=False, stop=True)
                mm.then_inc(s_sel, 1)

                for s in range(S):
                    w = W_OF[s]
                    rank = bank[4 + s % 2][:, 0:(Q + 1) * B].rearrange("p (k b) -> p k b", b=B)
                    e.wait_ge(s_ob4, through(step(g, s)))
                    e.wait_ge(s_run, through(before(g, s)))
                    nc.tensor.matmul(rank[:, 0:w + 1, :], ones_b[0:1, :], zeros_b[:, 0:(w + 1) * B],
                                     start=True, stop=False)
                    for k in range(w):
                        nc.tensor.matmul(rank[:, k, :], upper[:, :], ob[:, s % 2, k, :],
                                         start=False, stop=False)
                        n = w - k
                        mm = nc.tensor.matmul(rank[:, k + 1:w + 1, :], ones_b[:, :],
                                              ob[:, s % 2, k:k + 1, :].to_broadcast([P, n, B]),
                                              start=False, stop=(k == w - 1))
                    mm.then_inc(s_pa, 1)
            over_groups(e, select_rows)

            e.wait_ge(s_rngld[1], 16)
            def sum_sorted(i, g, q):
                sum_by_node(e, v5, seen5, g, 2, msg[:, q, :, 0:D])
            over_groups(e, sum_sorted)
            def sum_hop(i, g, q):
                e.wait_ge(s_rows6[q], (i + 1) * (16 * K))
                sum_by_node(e, v6, seen6, g, 2, rows[:, q, :, :])
            over_groups(e, sum_hop)

            nc.tensor.transpose(bank[3][:, 0:D], w_sb[:, :, :].rearrange("p a f -> p (a f)"),
                                ident[0:D, 0:D]).then_inc(s_wT, 1)
            e.wait_ge(s_wTs, 1)
            def last_product(i, j, q):
                e.wait_ge(s_h2, pair_through(j))
                e.wait_ge(s_hTs, pair_through(j - 2))
                nc.tensor.transpose(bank[0][:, q * P:(q + 1) * P],
                                    hb[:, q, 0:P], ident[:, :]).then_inc(s_hT, 1)
                e.wait_ge(s_hTs, pair_through(j))
                e.wait_ge(s_res, pair_through(j - 2))
                for h in range(2):
                    o = bank[1 + q][:, h * D:(h + 1) * D]
                    nc.tensor.matmul(o, ones_f[:, :], b_r[:, :], start=True, stop=False)
                    mm = nc.tensor.matmul(o, eaT[:, q, :], wT[:, h, :],
                                          start=False, stop=True)
                mm.then_inc(s_lin, 1)
            over(e, NP, last_product)

        @block.vector
        def _(e):
            done = [0]

            def link(ins):
                done[0] += 1
                ins.then_inc(s_dv, 1)
                e.wait_ge(s_dv, done[0])

            seen, seen4, seen5, seen6 = (e.alloc_register(f"dve_visits{n}") for n in (2, 4, 5, 6))
            for r in (seen, seen4, seen5, seen6):
                e.reg_mov(r, 0)
            for s_of, n in ((s_nl, 2), (s_nc, 2), (s_lk, BIAS), (s_msg, BIAS), (s_ob, BIAS), (s_ob4, BIAS),
                            (s_pl, BIAS), (s_run, BIAS), (s_pm, BIAS), (s_pr, BIAS), (s_pi, 2), (s_free5, 2), (s_free6, 2),
                            (s_h2, 2), (s_res, 2)):
                e.sem_inc(s_of, n)
            for v in (v2, v5, v6):
                e.sem_inc(v.added, 1)
            nc.vector.memset(w1e[:, :, :], 0.0)
            nc.vector.memset(w2e[:, :, :], 0.0)
            nc.vector.memset(w1n[:, :, :], 0.0)
            nc.vector.memset(wT[:, :, :], 0.0)
            nc.vector.memset(X[:, B - 1, :], 0.0)
            nc.vector.memset(ea[:, :, :, :], 0.0).then_inc(s_wzero, 1)

            e.wait_ge(s_dg, 16)
            link(nc.vector.tensor_reduce(rng_f[0:G, 0:1], dst_g[0:G, :], AX.X, ALU.min))
            link(nc.vector.tensor_reduce(rng_f[0:G, 1:2], dst_g[0:G, :], AX.X, ALU.max))
            link(nc.vector.tensor_copy(rng_i[0:G, :], rng_f[0:G, :]))
            nc.vector.tensor_scalar(rng_i[0:G, :], rng_i[0:G, :], 7, None, ALU.arith_shift_right)\
                .then_inc(s_rngd, 1)
            link(nc.vector.memset(tab[:, :], 0.0))

            def node_values(i, j, q):
                e.wait_ge(s_nb, pair_through(j))
                e.wait_ge(s_n2, pair_through(j - 2))
                nc.vector.scalar_tensor_tensor(out=hl[:, q, :], in0=hb[:, q, :], scalar=SLOPE,
                                               in1=hb[:, q, :], op0=ALU.mult, op1=ALU.max).then_inc(s_nl, 1)
                e.wait_ge(s_n2, pair_through(j))
                nc.vector.tensor_copy(U[:, bass.ds(j * 2, 2), :],
                                      bank[3 + q][:, 0:2 * D].rearrange("p (b f) -> p b f", f=D))\
                    .then_inc(s_nc, 1)
            over(e, NP, node_values)

            e.wait_ge(s_ids, 32)
            e.wait_ge(s_const, 1)
            e.wait_ge(s_rngld[0], 16)

            def mark_buckets(s, q, signal):
                w = W_OF[s]
                nc.vector.tensor_tensor(ob[:, s % 2, 0:w, :],
                                        bucket[:, q, tiles(s)].unsqueeze(2).to_broadcast([P, w, B]),
                                        iota_n[:, 0:B].unsqueeze(1).to_broadcast([P, w, B]),
                                        ALU.is_equal).then_inc(signal, 1)

            def messages(i, g, q):
                def leaky(s):
                    parts, cols = (P, 2 * P) if W_OF[s] == Q else (D, P)
                    e.wait_ge(s_eb, through(step(g, s)))
                    e.wait_ge(s_l2, through(before(g, s)))
                    nc.vector.scalar_tensor_tensor(
                        out=hl[0:parts, s % 2, 0:cols], in0=hb[0:parts, s % 2, 0:cols], scalar=SLOPE,
                        in1=hb[0:parts, s % 2, 0:cols], op0=ALU.mult, op1=ALU.max).then_inc(s_lk, 1)

                nc.vector.tensor_scalar(bucket[:, q, :], src_cols(g), 7, None,
                                        ALU.arith_shift_right).then_inc(s_bk, 1)
                e.wait_ge(s_bk, g + 1)
                leaky(0)
                for s in range(S):
                    w = W_OF[s]
                    if s + 1 < S:
                        leaky(s + 1)
                    e.wait_ge(s_hist, through(before(g, s)))
                    mark_buckets(s, q, s_ob)
                    e.wait_ge(s_l2, through(step(g, s)))
                    e.wait_ge(s_rows[q][s], (i + 1) * (16 * w))
                    nc.vector.tensor_tensor(msg[:, q, tiles(s), 0:D],
                                            bank[3 + s % 2][:, 0:w * D].rearrange("p (k f) -> p k f", f=D),
                                            rows[:, q, tiles(s), :], ALU.mult).then_inc(s_msg, 1)
                mark_and_add(e, v2, seen, g, 0, dst_flat, tab, D + 1)
            over_groups(e, messages)

            e.wait_ge(v2.added, e.snap(seen) + 1)
            wide = [P, B, D]

            def spread(t):
                return t.unsqueeze(2).to_broadcast(wide)

            def norm(t, to, squares, n):
                link(nc.vector.tensor_reduce(mean[:, :], t, AX.X, ALU.add))
                link(nc.vector.tensor_scalar(mean[:, :], mean[:, :], 1.0 / D, None, ALU.mult))
                link(nc.vector.tensor_tensor(t, t, spread(mean[:, :]), ALU.subtract))
                link(nc.vector.tensor_tensor(squares, t, t, ALU.mult))
                link(nc.vector.tensor_reduce(var[:, :], squares, AX.X, ALU.add))
                nc.vector.tensor_scalar(var[:, :], var[:, :], 1.0 / D, EPS, ALU.mult, ALU.add)\
                    .then_inc(s_var, 1)
                e.wait_ge(s_dev, n + 1)
                link(nc.vector.reciprocal(std[:, :], std[:, :]))
                link(nc.vector.tensor_tensor(to, t, spread(std[:, :]), ALU.mult))

            e.wait_ge(s_load, 16 * N_LOADS)
            e.wait_ge(s_xld, 32)
            e.wait_ge(s_nst, 16)
            nc.vector.tensor_scalar(var[:, :], agg0[:, :, D], 1.0, None, ALU.add).then_inc(s_var, 1)
            link(nc.vector.tensor_tensor(scale[:, :], scl[:, 0:1], scl[:, 1:2], ALU.mult))
            link(nc.vector.scalar_tensor_tensor(out=U[:, :, :], in0=agg0[:, :, 0:D], scalar=scale[:, 0:1],
                                                in1=X[:, :, :], op0=ALU.mult, op1=ALU.add))
            e.wait_ge(s_dev, 1)
            link(nc.vector.reciprocal(dinv[:, :], std[:, :]))
            norm(U[:, :, :], U[:, :, :], H[:, :, :], 1)
            link(nc.vector.tensor_tensor(U[:, :, :], U[:, :, :], gam[:, :].unsqueeze(1).to_broadcast(wide), ALU.mult))
            link(nc.vector.tensor_tensor(U[:, :, :], U[:, :, :], bet[:, :].unsqueeze(1).to_broadcast(wide), ALU.add))
            link(nc.vector.tensor_tensor(U[:, :, :], U[:, :, :], X[:, :, :], ALU.add))
            norm(U[:, :, :], X[:, :, :], H[:, :, :], 2)
            nc.vector.tensor_tensor(U[:, :, :], X[:, :, :], spread(dinv[:, :]), ALU.mult)
            nc.vector.memset(H[:, :, :], 0.0)
            e.wait_ge(s_total, 1)
            nc.vector.tensor_copy(count_b[:, :], bank[6][:, 0:B]).then_inc(s_cT, 1)
            e.wait_ge(s_cT, 2)
            nc.vector.tensor_copy(counts_T[0:B, :], bank[7][0:B, 0:P]).then_inc(s_cTs, 1)
            e.wait_ge(s_bases, 1)
            link(nc.vector.tensor_copy(base_b[:, :], bank[6][:, 0:B]))
            for a in range(2):
                link(nc.vector.tensor_scalar(cmp_w[0:G, a, 0:B - 1], base_b[0:G, 1:B], thr[0:G, a:a + 1],
                                             None, ALU.is_le))
            link(nc.vector.tensor_reduce(rng_f[0:G, :], cmp_w[0:G, :, 0:B - 1], AX.X, ALU.add))
            nc.vector.tensor_copy(rng_i[0:G, :], rng_f[0:G, :]).then_inc(s_rngd, 1)
            e.sem_inc(s_g1, 1)

            def marks_and_places(i, g, q):
                e.wait_ge(s_row[q], (i + 1) * 16)
                by_tile = dst_row[:, q, :].rearrange("p (e k) -> p k e", k=K)
                lo, hi = block_range(e, g, 0)
                with e.Fori(lo, hi + 1) as blk:
                    n = e.snap(seen4)
                    for s in range(S):
                        e.wait_ge(s_u4[s], n + 1)
                        nc.vector.tensor_scalar(OH[:, tiles(s), :], by_tile[:, tiles(s), :],
                                                node_id[:, bass.ds(blk, 1)], None,
                                                ALU.is_equal).then_inc(s_m4[s], 1)
                    e.reg_add(seen4, seen4, 1)

                nc.vector.tensor_scalar(bucket[:, q, :], src_cols(g), 7, None,
                                        ALU.arith_shift_right).then_inc(s_bk4, 1)
                e.wait_ge(s_bk4, g + 1)
                e.wait_ge(s_pa, through(before(g, 0)))
                mark_buckets(0, q, s_ob4)
                for s in range(S):
                    w = W_OF[s]
                    if s + 1 < S:
                        e.wait_ge(s_pa, through(before(g, s + 1)))
                        mark_buckets(s + 1, q, s_ob4)
                    rank = bank[4 + s % 2][:, 0:(Q + 1) * B].rearrange("p (k b) -> p k b", b=B)
                    e.wait_ge(s_pa, through(step(g, s)))
                    e.wait_ge(s_run, through(step(g, s) - 1))
                    e.wait_ge(s_pr, through(step(g, s) - 1))
                    nc.vector.tensor_tensor(rank_w[:, 0:w, :], rank[:, 0:w, :],
                                            base_b[:, :].unsqueeze(1).to_broadcast([P, w, B]),
                                            ALU.add).then_inc(s_pl, 1)
                    e.wait_ge(s_pl, through(step(g, s)))
                    nc.vector.tensor_tensor(base_b[:, :], base_b[:, :], rank[:, w, :],
                                            ALU.add).then_inc(s_run, 1)
                    nc.vector.tensor_tensor(rank_w[:, 0:w, :], rank_w[:, 0:w, :], ob[:, s % 2, 0:w, :],
                                            ALU.mult).then_inc(s_pm, 1)
                    e.wait_ge(s_pm, through(step(g, s)))
                    nc.vector.tensor_reduce(pos_f[:, q, tiles(s)], rank_w[:, 0:w, :], AX.X, ALU.add)\
                        .then_inc(s_pr, 1)
                e.wait_ge(s_pr, through(step(g, S - 1)))
                e.wait_ge(s_rec, g + 2)
                nc.vector.tensor_copy(pos_i[:, q, :], pos_f[:, q, :]).then_inc(s_pi, 1)
            over_groups(e, marks_and_places)

            e.wait_ge(s_rngld[1], 16)
            def keep_and_mark(i, g, q):
                e.wait_ge(s_m[q], (i + 1) * 16)
                nc.vector.tensor_copy(src_cols(g).unsqueeze(2), msg[:, q, :, D:D + 1].bitcast(i32))
                nc.vector.tensor_copy(dst_cols(g).unsqueeze(2), msg[:, q, :, D + 1:R].bitcast(i32))\
                    .then_inc(s_srt, 1)
                e.wait_ge(s_srt, g + 1)
                mark_and_add(e, v5, seen5, g, 2, src_flat, H_flat, D)
                e.sem_inc(s_free5, 1)
            over_groups(e, keep_and_mark)
            e.wait_ge(v5.added, e.snap(seen5) + 1)
            link(nc.vector.tensor_tensor(H[:, :, :], H[:, :, :], U[:, :, :], ALU.add))
            link(nc.vector.tensor_tensor(H[:, :, :], H[:, :, :], spread(dinv[:, :]), ALU.mult))
            link(nc.vector.tensor_tensor(U[:, :, :], H[:, :, :], spread(dinv[:, :]), ALU.mult))
            nc.vector.memset(H[:, :, :], 0.0).then_inc(s_g2, 1)

            def mark_hop(i, g, q):
                mark_and_add(e, v6, seen6, g, 2, src_flat, H_flat, D)
                e.sem_inc(s_free6, 1)
            over_groups(e, mark_hop)
            e.wait_ge(v6.added, e.snap(seen6) + 1)
            e.sem_inc(s_turn["vector"], 1)

            def h2_and_residual(i, j, q):
                pair = bass.ds(j * 2, 2)
                h2 = hb[:, q, 0:P].rearrange("p (b f) -> p b f", f=D)
                e.wait_ge(s_hT, pair_through(j - 2))
                nc.vector.tensor_tensor(h2, H[:, pair, :], U[:, pair, :], ALU.add).then_inc(s_ha, 1)
                e.wait_ge(s_ha, j + 1)
                nc.vector.tensor_tensor(h2, h2, dinv[:, pair].unsqueeze(2).to_broadcast([P, 2, D]),
                                        ALU.mult).then_inc(s_h2, 1)
                e.wait_ge(s_lin, pair_through(j))
                nc.vector.tensor_tensor(H[:, pair, :], X[:, pair, :],
                                        bank[1 + q][:, 0:P].rearrange("p (b f) -> p b f", f=D),
                                        ALU.add).then_inc(s_res, 1)
            over(e, NP, h2_and_residual)
            e.wait_ge(s_res, pair_through(NP - 1))
            norm(H[:, :, :], H[:, :, :], U[:, :, :], 3)
            e.sem_inc(s_fin, 1)


_INS = ['x', 'src', 'dst', 'edge_attr_32', 'L0_gnn_W1n', 'L0_gnn_b1n', 'L0_gnn_W2n', 'L0_gnn_b2n',
        'L0_gnn_W1e', 'L0_gnn_b1e', 'L0_gnn_W2e', 'L0_gnn_b2e', 'L0_gnn_res_w', 'L0_gnn_dp_scale',
        'L0_gnn_gamma', 'L0_gnn_beta', 'L1_gnn_W', 'L1_gnn_b']


def kernel(**inputs):
    import numpy as np
    import concourse.bacc as bacc
    from concourse.bass_utils import run_bass_kernel_spmd

    nc = bacc.Bacc("TRN2", target_bir_lowering=False, num_devices=1)
    arrays, args = {}, []
    for name in _INS:
        a = np.ascontiguousarray(inputs[name])
        arrays[f"in_{name}"] = a
        args.append(nc.dram_tensor(f"in_{name}", a.shape, mybir.dt.from_np(a.dtype), kind="ExternalInput").ap())
    out = nc.dram_tensor("out", inputs["x"].shape, mybir.dt.float32, kind="ExternalOutput").ap()
    gnn_two_layers(nc, *args, out)
    r = run_bass_kernel_spmd(nc, [arrays], core_ids=[0])
    return r.results[0]["out"]
```

```python
import concourse.bass as bass
from concourse import mybir
from contextlib import ExitStack


def gnn_two_layers(nc, x, src, dst, edge_attr, W1n, b1n, W2n, b2n, W1e, b1e, W2e, b2e,
                   res_w, dp_scale, gamma, beta, W, b, out):
    f32, i32, bf16 = mybir.dt.float32, mybir.dt.int32, mybir.dt.bfloat16
    ALU, ACT, AX = mybir.AluOpType, mybir.ActivationFunctionType, mybir.AxisListType

    P = 128
    N, D = x.shape
    E, DE = edge_attr.shape
    HN = W1n.shape[1]
    EPS = 1e-5
    SLOPE = 0.1
    K = 25
    GE = K * P
    G = E // GE
    assert G * GE == E and HN == P and D == 64 and DE == 32
    B = -(-N // P)
    NL = N - (B - 1) * P
    R = D + 2
    Q = 4
    S = -(-K // Q)
    W_OF = [min(Q, K - Q * s) for s in range(S)]
    BIAS = 2 * S
    BP = B
    NP = B // 2
    assert B % 2 == 0 and NP % 2 == 1
    assert B * Q <= 512 and S == 7 and G % 2 == 1 and B < 128

    ctx = ExitStack()
    with ctx:
        def sb(name, shape, dt=f32):
            return ctx.enter_context(nc.sbuf_tensor(name, shape, dt))

        def sem(name):
            return ctx.enter_context(nc.semaphore(name))

        node_rows = nc.dram_tensor("node_rows", [BP * P, D], f32).ap()
        hop_rows = nc.dram_tensor("hop_rows", [BP * P, D], f32).ap()
        sorted_rows = nc.dram_tensor("sorted_rows", [E, R], f32).ap()
        range_dram = nc.dram_tensor("range_dram", [2, P], i32).ap()

        X = sb("X", [P, BP, D])
        TAB_W = max((B + 1) * (D + 1), 2 * GE)
        tab = sb("tab", [P, TAB_W])
        agg0 = tab[:, 0:B * (D + 1)].rearrange("p (b f) -> p b f", f=D + 1)
        dst_row = tab[:, 0:2 * GE].bitcast(i32).rearrange("p (q e) -> p q e", q=2)
        U = sb("U", [P, BP, D])
        H_all = sb("H", [P, B + 1, D])
        H = H_all[:, 0:B, :]
        src_i = sb("src_i", [P, G, K], i32)
        dst_i = sb("dst_i", [P, G, K], i32)
        ea = sb("ea", [P, 2, K, DE])
        eaT = sb("eaT", [P, 4, P])
        hb = sb("hb", [P, 4, 2 * P])
        hl = sb("hl", [P, 4, 2 * P])
        rows = sb("rows", [P, 2, K, D])
        msg = sb("msg", [P, 2, K, R])
        OH = sb("OH", [P, K, P])
        ob = sb("ob", [P, 3, Q, B], bf16)
        rank_w = sb("rank_w", [P, 3, Q, B])
        idx = sb("idx", [P, 2, K], i32)
        bucket = sb("bucket", [P, 2, K], i32)
        pos_f = sb("pos_f", [P, 2, K])
        pos_i = sb("pos_i", [P, 2, K], i32)
        iota_n = sb("iota_n", [P, P])
        block0 = sb("block0", [P, B + 1])
        node_id = sb("node_id", [P, BP])
        ident = sb("ident", [P, P])
        upper = sb("upper", [P, P], bf16)
        upper_f = sb("upper_f", [P, P])
        counts_T = sb("counts_T", [P, P])
        ones_b = sb("ones_b", [P, P], bf16)
        zeros_b = sb("zeros_b", [1, 512], bf16)
        assert (Q + 1) * B <= 512
        ones_f = sb("ones_f", [1, P])
        w1n = sb("w1n", [P, 2, P])
        w2n = sb("w2n", [P, D])
        b1n_c = sb("b1n_c", [P, 1])
        b2n_r = sb("b2n_r", [1, D])
        w1e = sb("w1e", [P, 2, P])
        w2e = sb("w2e", [P, 2, D])
        b1e_c = sb("b1e_c", [P, 1])
        b2e_f = sb("b2e_f", [3, D])
        b2e_p = sb("b2e_p", [3, 3, D], bf16)
        b2e_3 = sb("b2e_3", [3, D], bf16)
        w_sb = sb("w_sb", [D, 2, D])
        wT = sb("wT", [P, 2, D])
        b_r = sb("b_r", [1, D])
        gam = sb("gam", [P, D])
        bet = sb("bet", [P, D])
        scl = sb("scl", [P, 2])
        scale = sb("scale", [P, 1])
        mean = sb("mean", [P, BP])
        var = sb("var", [P, BP])
        std = sb("std", [P, BP])
        dinv = sb("dinv", [P, BP])
        place = sb("place", [P, 2, B])
        thr = sb("thr", [P, 2])
        cmp_w = sb("cmp_w", [P, 2, B])
        rng_f = sb("rng_f", [P, 2])
        rng_i = sb("rng_i", [P, 2], i32)
        dst_g = OH[:, :, :].rearrange("p k e -> p (k e)").bitcast(i32)
        rng_d = sb("rng_d", [1, 2, P], i32)

        bank = [ctx.enter_context(nc.psum_tensor(f"bank{i}", [P, 512], f32)) for i in range(6)]
        sums = ctx.enter_context(nc.psum_tensor("sums", [P, 2, 512], f32))

        s_turn = {k: sem(f"{k}_turns") for k in ("sync", "gpsimd", "vector")}
        s_fill = sem("fills_landed")
        s_const = sem("constants_made")
        s_wzero = sem("weight_tiles_zeroed")
        s_load = sem("weights_loaded")
        s_xld = sem("x_loaded")
        s_ids = sem("indices_loaded")
        s_dg = sem("dst_groups_loaded")
        s_dv = sem("vector_op_done")
        s_rngd = sem("ranges_made")
        s_rngst = sem("ranges_stored")
        s_rngld = [sem("dst_ranges_loaded"), sem("src_ranges_loaded")]
        s_xr = [sem(f"x_pair_in{q}") for q in range(2)]
        s_xT = sem("x_transposed")
        s_xTs = sem("x_transpose_copied")
        s_n1 = sem("node_layer1_done")
        s_nb = sem("node_bias_done")
        s_nl = sem("node_leaky_done")
        s_n2 = sem("node_layer2_done")
        s_nc = sem("node_rows_copied")
        s_nst = sem("node_rows_stored")
        s_ea = [sem(f"edge_features_in{q}") for q in range(2)]
        s_idx = [sem(f"src_indices_in{q}") for q in range(2)]
        s_ix6 = sem("dst_indices_copied")
        s_tp = sem("edge_transposed")
        s_tc = sem("edge_transpose_copied")
        s_l1 = sem("edge_layer1_done")
        s_eb = sem("edge_bias_done")
        s_lk = sem("edge_leaky_done")
        s_l2 = sem("edge_layer2_done")
        s_b3 = sem("edge_bias_parts_made")
        s_msg = sem("messages_made")
        s_bk = sem("bucket_ids_made")
        s_ob = sem("buckets_marked")
        s_hist = sem("buckets_counted")
        s_total = sem("bucket_totals_ready")
        s_rows = [[sem(f"rows_gathered{q}_{s}") for s in range(S)] for q in range(2)]
        s_var = sem("variance_made")
        s_dev = sem("deviation_made")
        s_cT = sem("counts_spread")
        s_bases = sem("bases_summed")
        s_g1 = sem("stage3_done")
        s_row = [sem(f"dst_row_in{q}") for q in range(2)]
        s_m4 = [sem(f"node_marks{i}") for i in range(S)]
        s_u4 = [sem(f"node_marks_used{i}") for i in range(S)]
        s_sel = sem("group_rows_selected")
        s_rec = sem("group_rows_copied")
        s_bk4 = sem("bucket_ids_made_again")
        s_ob4 = sem("buckets_marked_again")
        s_pa = sem("ranks_ready")
        s_pl = sem("places_of_blocks_added")
        s_run = sem("next_places_advanced")
        s_pm = sem("ranks_picked")
        s_pr = sem("positions_summed")
        s_pi = sem("positions_rounded")
        s_sc = [sem(f"rows_scattered{q}") for q in range(2)]
        s_m = [sem(f"sorted_rows_in{q}") for q in range(2)]
        s_srt = sem("sorted_ids_kept")
        s_free5 = sem("stage5_group_summed")
        s_g2 = sem("hop_rows_made")
        s_g2st = sem("hop_rows_stored")
        s_rows6 = [sem(f"hop_rows_gathered{q}") for q in range(2)]
        s_free6 = sem("stage6_group_summed")
        s_wT = sem("W_transposed")
        s_wTs = sem("W_transpose_copied")
        s_ha = sem("hop_sum_with_loop")
        s_h2 = sem("h2_made")
        s_hT = sem("h2_transposed")
        s_hTs = sem("h2_transpose_copied")
        s_lin = sem("last_product_done")
        s_res = sem("residual_added")
        s_fin = sem("output_made")
        s_out = sem("output_stored")

        class Visits:

            def __init__(self, tag):
                self.marks = [sem(f"{tag}_marks{s}") for s in range(S)]
                self.used = [sem(f"{tag}_used{s}") for s in range(S)]
                self.added = sem(f"{tag}_added")

        v2, v5, v6 = Visits("dst"), Visits("src1"), Visits("src2")

        block = ctx.enter_context(nc.Block())

        def step(g, s):
            return g * S + s

        def through(n):
            return n + (1 + BIAS)

        def before(g, s):
            return step(g, s) - (1 if s == 0 else 2)

        def before4(g, s):
            return step(g, s) - (4 if s >= 4 else 7 if s == 3 else 3)

        def hidden(s):
            return bank[1 + s % 2]

        def edge_out(s):
            return bank[3 + s % 2]

        def ahead(g, q, s):
            if s < S:
                return g, q, s
            return None if isinstance(g, int) and g == G - 1 else (g + 1, 1 - q, s - S)

        def tiles(s):
            return slice(Q * s, Q * s + W_OF[s])

        def over(e, count, body, apart=0):
            for i in range(apart):
                body(i, 2 * i, 0)
                body(i, 2 * i + 1, 1)
            with e.Fori(apart, count // 2) as i:
                body(i, i * 2, 0)
                body(i, i * 2 + 1, 1)
            if count % 2:
                body(count // 2, count - 1, 0)

        def over_groups(e, body, apart=0):
            over(e, G, body, apart)

        def pair_through(j):
            return j + 3

        def block_range(e, g, which):
            both = e.value_load(rng_d[0:1, which, bass.ds(g, 1)], min_val=0, max_val=257 * (B - 1))
            return (e.snap(both & 255, min_val=0, max_val=B - 1),
                    e.snap(both >> 8, min_val=0, max_val=B - 1))

        N_LOADS = 21
        src_flat = src_i[:, :, :].rearrange("p g k -> p (g k)")
        dst_flat = dst_i[:, :, :].rearrange("p g k -> p (g k)")
        H_flat = H_all[:, :, :].rearrange("p b f -> p (b f)")

        def src_cols(g):
            return src_flat[:, bass.ds(g * K, K)]

        def dst_cols(g):
            return dst_flat[:, bass.ds(g * K, K)]

        def a_block(value):
            return nc.s_assert_within(value, 0, B - 1, skip_runtime_bounds_check_because=
                                      "the ranges hold block numbers of the nodes of edges")

        def mark_and_add(e, v, regs, g, q, which, ids, table, width):
            seen, last_blk, last_row = regs
            lo, hi = block_range(e, g, which)
            with e.Fori(lo, hi + 1, 2) as blk:
                n = e.snap(seen)
                blk = a_block(blk)
                for half in range(2):
                    for s in range(S):
                        w = W_OF[s]
                        e.wait_ge(v.used[s], n * 2 + (half + 1))
                        nc.vector.scalar_tensor_tensor(
                            out=OH[:, tiles(s), :],
                            in0=ids[:, bass.ds(g * K + Q * s, w)].unsqueeze(2).to_broadcast([P, w, P]),
                            scalar=block0[:, bass.ds(blk + half, 1)],
                            in1=iota_n[:, :].unsqueeze(1).to_broadcast([P, w, P]),
                            op0=ALU.subtract, op1=ALU.is_equal).then_inc(v.marks[s], 1)
                    if half == 0:
                        add_last(e, v, n, last_blk, last_row, table, width)
                e.reg_mov(last_row, q)
                e.reg_mov(last_blk, blk)
                e.reg_add(seen, seen, 1)

        def add_last(e, v, n, last_blk, last_row, table, width):
            first = e.snap(last_blk, min_val=0, max_val=B - 1) * width
            row = sums[:, bass.ds(e.snap(last_row, min_val=0, max_val=1), 1), 0:2 * width]
            e.wait_ge(v.used[S - 1], n * 2 + 1)
            e.wait_ge(v.added, n + 1)
            part = table[:, bass.ds(first, 2 * width)]
            nc.vector.tensor_tensor(part, part, row.rearrange("p a f -> p (a f)"), ALU.add)\
                .then_inc(v.added, 1)

        def sum_by_node(e, v, regs, g, q, which, data):
            seen, free = regs
            lo, hi = block_range(e, g, which)
            width = data.shape[2]
            e.reg_add(free, seen, 1)
            with e.Fori(lo, hi + 1, 2):
                n = e.snap(seen)
                e.wait_ge(v.added, e.snap(free))
                for half in range(2):
                    for s in range(S):
                        e.wait_ge(v.marks[s], n * 2 + (half + 1))
                        for k in range(Q * s, Q * s + W_OF[s]):
                            mm = nc.tensor.matmul(sums[:, q, half * width:(half + 1) * width],
                                                  OH[:, k, :], data[:, k, :],
                                                  start=(k == 0), stop=(k == K - 1))
                        mm.then_inc(v.used[s], 1)
                e.reg_add(seen, seen, 1)
                e.reg_add(free, seen, 2)

        def group_summed(signal):
            nc.tensor.matmul(bank[5][0:1, 0:1], ones_b[0:1, 0:1], zeros_b[:, 0:1], start=True, stop=True)\
                .then_inc(signal, 1)

        def open_sums(e, v, width):
            for s in range(S - 1):
                e.sem_inc(v.used[s], 1)
            nc.tensor.matmul(sums[:, 1, 0:2 * width], ones_b[0:1, :], zeros_b[:, 0:2 * width],
                             start=True, stop=True).then_inc(v.used[S - 1], 1)

        def row_of(v, n):
            return v.rearrange("(a n) -> a n", a=1) if n is None else \
                v.rearrange("(a n) -> a n", a=1).to_broadcast([n, v.shape[0]])

        @block.sync
        def _(e):
            e.dma_start(dst_g[0:G, :], dst.rearrange("(g e) -> g e", e=GE)).then_inc(s_dg, 16)
            e.wait_ge(s_wzero, 1)
            e.dma_start(X[:, 0:B - 1, :],
                        x[0:(B - 1) * P, :].rearrange("(b p) f -> p b f", p=P)).then_inc(s_xld, 16)
            e.dma_start(X[0:NL, B - 1, :], x[(B - 1) * P:N, :]).then_inc(s_xld, 16)
            for i_sb, i_dr in ((src_i, src), (dst_i, dst)):
                e.dma_start(i_sb[:, :, :], i_dr.rearrange("(g p k) -> p g k", p=P, k=K)).then_inc(s_ids, 16)

            def spread_ranges(n):
                e.wait_ge(s_rngd, n + 1)
                e.dma_start(range_dram[n:n + 1, 0:G].rearrange("a g -> g a"), rng_i[0:G, 0:1])\
                    .then_inc(s_rngst, 16)
                e.wait_ge(s_rngst, 16 * (n + 1))
                e.dma_start(rng_d[0:1, n, 0:G], range_dram[n:n + 1, 0:G]).then_inc(s_rngld[n], 16)
            spread_ranges(0)

            def load_pair(i, j, q):
                e.wait_ge(s_xT, pair_through(j - 2))
                slot = ea[:, q, 0:4, :].rearrange("p k f -> p (k f)").rearrange("p (b f) -> p b f", b=2)
                if isinstance(j, int) and j == NP - 1:
                    e.dma_start(slot[:, 0, :], x[(B - 2) * P:(B - 1) * P, :]).then_inc(s_xr[q], 16)
                    e.dma_start(slot[0:NL, 1, :], x[(B - 1) * P:N, :]).then_inc(s_xr[q], 16)
                else:
                    e.dma_start(slot, x[bass.ds(j * (2 * P), 2 * P), :]
                                .rearrange("(b p) f -> p b f", p=P)).then_inc(s_xr[q], 16)
            over(e, NP, load_pair)

            e.wait_ge(s_nc, pair_through(NP - 1))
            e.dma_start(node_rows.rearrange("(b p) f -> p b f", p=P), U[:, :, :]).then_inc(s_nst, 16)

            def load_features(i, g, q):
                first = e.snap(g * GE)
                e.wait_ge(s_tp, through(step(g - 2, S - 1)))
                e.dma_start(ea[:, q, :, :],
                            edge_attr[bass.ds(first, GE), :].rearrange("(p k) f -> p k f", k=K))\
                    .then_inc(s_ea[q], 16)
                e.wait_ge(s_msg, through(step(g - 2, S - 1)))
                e.sem_inc(s_turn["sync"], 1)
                e.dma_start(idx[:, q, :], src[bass.ds(first, GE)].rearrange("(p k) -> p k", k=K))\
                    .then_inc(s_idx[q], 16)
            over_groups(e, load_features)

            spread_ranges(1)

            e.wait_ge(s_g1, 1)
            def load_dst_row(i, g, q):
                first = e.snap(g * GE)
                e.wait_ge(s_pi, g + 1)
                e.dma_start(dst_row[:, q, :], dst[bass.ds(first, GE)]
                            .rearrange("(a e) -> a e", a=1).to_broadcast([P, GE])).then_inc(s_row[q], 16)
            over_groups(e, load_dst_row)

            for q in range(2):
                e.wait_ge(s_sc[q], 16 * K * ((G + 1 - q) // 2))
            def load_sorted(i, g, q):
                first = e.snap(g * GE)
                e.wait_ge(s_free5, g + 1)
                e.dma_start(msg[:, q, :, :],
                            sorted_rows[bass.ds(first, GE), :].rearrange("(p k) f -> p k f", k=K))\
                    .then_inc(s_m[q], 16)
            over_groups(e, load_sorted)
            e.wait_ge(s_g2, 1)
            e.dma_start(hop_rows.rearrange("(b p) f -> p b f", p=P), U[:, :, :]).then_inc(s_g2st, 16)

            e.wait_ge(s_fin, 1)
            e.dma_start(out[0:(B - 1) * P, :].rearrange("(b p) f -> p b f", p=P), H[:, 0:B - 1, :])\
                .then_inc(s_out, 16)
            e.dma_start(out[(B - 1) * P:N, :], H[0:NL, B - 1, :]).then_inc(s_out, 16)
            e.wait_ge(s_out, 32)

        @block.gpsimd
        def _(e):
            e.memset(ident[:, :], 0.0).then_inc(s_fill, 1)
            e.memset(upper_f[:, :], 1.0).then_inc(s_fill, 1)
            e.memset(ones_b[:, :], 1.0).then_inc(s_fill, 1)
            e.memset(zeros_b[:, :], 0.0)
            e.memset(ones_f[:, :], 1.0)
            for q in range(2):
                e.memset(msg[:, q, :, :], 1.0)
            small = dict(channel_multiplier=0, allow_small_or_imprecise_dtypes=True)
            e.iota(iota_n[:, :], [[1, P]], base=0, **small)
            e.iota(block0[:, :], [[P, B + 1]], base=0, **small)
            lanes = dict(allow_small_or_imprecise_dtypes=True)
            e.iota(node_id[:, :], [[P, B]], base=0, channel_multiplier=1, **lanes)
            e.iota(thr[:, 0:1], [[0, 1]], base=0, channel_multiplier=GE, **lanes)
            e.iota(thr[:, 1:2], [[0, 1]], base=GE - 1, channel_multiplier=GE, **lanes)
            e.wait_ge(s_fill, 3)
            e.affine_select(out=ident[:, :], in_=ident[:, :], compare_op=ALU.not_equal, fill=1.0,
                            base=0, pattern=[[-1, P]], channel_multiplier=1)
            e.affine_select(out=upper[:, :], in_=ones_b[:, :], compare_op=ALU.is_gt, fill=0.0,
                            base=0, pattern=[[1, P]], channel_multiplier=-1)
            e.affine_select(out=upper_f[:, :], in_=upper_f[:, :], compare_op=ALU.is_gt, fill=0.0,
                            base=0, pattern=[[1, P]], channel_multiplier=-1).then_inc(s_const, 1)

            e.wait_ge(s_ids, 32)
            def gather_nodes(i, g, q):
                e.wait_ge(s_msg, through(step(g - 2, S - 1)))
                e.wait_ge(s_idx[q], (i + 1) * 16)
                e.wait_ge(s_nst, 16)
                e.sem_inc(s_turn["gpsimd"], 1)
                for k in range(K):
                    e.indirect_dma_start(
                        out=rows[:, q, k, :], out_offset=None, in_=node_rows,
                        in_offset=bass.IndirectOffsetOnAxis(ap=idx[:, q, k:k + 1], axis=0),
                    ).then_inc(s_rows[q][k // Q], 16)
            over_groups(e, gather_nodes)

            def scatter_rows(i, g, q):
                e.wait_ge(s_rec, g + 2)
                e.wait_ge(s_pi, g + 3)
                e.sem_inc(s_turn["gpsimd"], 1)
                for k in range(K):
                    e.indirect_dma_start(
                        out=sorted_rows,
                        out_offset=bass.IndirectOffsetOnAxis(ap=pos_i[:, q, k:k + 1], axis=0),
                        in_=msg[:, q, k, :], in_offset=None).then_inc(s_sc[q], 16)
            over_groups(e, scatter_rows)

            def gather_hop(i, g, q):
                e.wait_ge(s_free6, g + 1)
                e.wait_ge(s_ix6, g + 1)
                e.wait_ge(s_g2st, 16)
                e.sem_inc(s_turn["gpsimd"], 1)
                for k in range(K):
                    e.indirect_dma_start(
                        out=rows[:, q, k, :], out_offset=None, in_=hop_rows,
                        in_offset=bass.IndirectOffsetOnAxis(ap=idx[:, q, k:k + 1], axis=0),
                    ).then_inc(s_rows6[q], 16)
            over_groups(e, gather_hop)

        @block.scalar
        def _(e):
            e.wait_ge(s_wzero, 1)
            loads = [(w1n[0:D, 0, :], W1n), (w1n[D:P, 1, :], W1n), (w2n[:, :], W2n),
                     (b1n_c[:, :], b1n.rearrange("(n a) -> n a", a=1)), (b2n_r[:, :], row_of(b2n, None)),
                     (w2e[0:D, 0, :], W2e), (w2e[D:P, 1, :], W2e), (b2e_f[:, :], row_of(b2e, 3)),
                     (b1e_c[0:D, :], b1e.rearrange("(n a) -> n a", a=1)),
                     (b1e_c[D:P, :], b1e.rearrange("(n a) -> n a", a=1)),
                     (w_sb[:, 0, :], W), (w_sb[:, 1, :], W), (b_r[:, :], row_of(b, None)),
                     (gam[:, :], row_of(gamma, P)), (bet[:, :], row_of(beta, P)),
                     (scl[:, 0:1], row_of(dp_scale, P)), (scl[:, 1:2], row_of(res_w, P))]
            for t in range(Q):
                loads.append((w1e[DE * t:DE * (t + 1), t // 2, D * (t % 2):D * (t % 2) + D], W1e))
            assert len(loads) == N_LOADS
            for to, of in loads:
                e.dma_start(to, of).then_inc(s_load, 16)

            e.sem_inc(s_xTs, 2)
            e.sem_inc(s_nb, 2)
            e.wait_ge(s_load, 16 * N_LOADS)
            def node_copies(i, j, q):
                e.wait_ge(s_xT, pair_through(j))
                e.wait_ge(s_n1, pair_through(j - 2))
                nc.scalar.activation(eaT[:, q, :], bank[0][:, q * P:(q + 1) * P],
                                     ACT.Copy).then_inc(s_xTs, 1)
                e.wait_ge(s_n1, pair_through(j))
                e.wait_ge(s_nl, pair_through(j - 2))
                nc.scalar.activation(hb[:, q, :], bank[1 + q][:, 0:2 * P], ACT.Identity,
                                     bias=b1n_c[:, :]).then_inc(s_nb, 1)
            over(e, NP, node_copies)

            e.sem_inc(s_tc, BIAS)
            e.sem_inc(s_eb, BIAS)
            def copy_transpose(g, s):
                w = W_OF[s] * DE
                e.wait_ge(s_tp, through(step(g, s)))
                e.wait_ge(s_l1, through(before4(g, s)))
                nc.scalar.activation(eaT[0:w, s % 4, :], bank[0][0:w, 0:P], ACT.Copy).then_inc(s_tc, 1)

            def add_bias(g, s):
                parts, cols = (P, 2 * P) if W_OF[s] == Q else (D, P)
                e.wait_ge(s_l1, through(step(g, s)))
                e.wait_ge(s_lk, through(before4(g, s)))
                nc.scalar.activation(hb[0:parts, s % 4, 0:cols], hidden(s)[0:parts, 0:cols],
                                     ACT.Identity, bias=b1e_c[0:parts, :]).then_inc(s_eb, 1)

            copy_transpose(0, 0)
            copy_transpose(0, 1)
            add_bias(0, 0)
            copy_transpose(0, 2)
            add_bias(0, 1)
            def edge_copies(i, g, q):
                for s in range(S):
                    if (t := ahead(g, q, s + 3)) is not None:
                        copy_transpose(t[0], t[2])
                    if (t := ahead(g, q, s + 2)) is not None:
                        add_bias(t[0], t[2])
            over_groups(e, edge_copies)

            def deviation(n):
                e.wait_ge(s_var, n + 1)
                nc.scalar.activation(std[:, :], var[:, :], ACT.Sqrt).then_inc(s_dev, 1)
            for n in range(3):
                deviation(n)

            e.sem_inc(s_rec, 1)
            def rows_out(i, g, q):
                if not isinstance(i, int) or i > 0:
                    e.wait_ge(s_sc[q], i * (16 * K))
                nc.scalar.activation(msg[:, q, :, D:D + 1].bitcast(i32), src_cols(g).unsqueeze(2), ACT.Copy)
                nc.scalar.activation(msg[:, q, :, D + 1:R].bitcast(i32), dst_cols(g).unsqueeze(2), ACT.Copy)
                e.wait_ge(s_sel, g + 1)
                for c in range(4):
                    w = min(8, K - 8 * c)
                    last = nc.scalar.activation(
                        msg[:, q, 8 * c:8 * c + w, 0:D],
                        bank[c][:, 0:w * D].rearrange("p (k f) -> p k f", f=D), ACT.Copy)
                last.then_inc(s_rec, 1)
            over_groups(e, rows_out, apart=1)

            def copy_indices(i, g, q):
                e.wait_ge(s_free6, g + 1)
                nc.scalar.activation(idx[:, q, :], dst_cols(g), ACT.Copy).then_inc(s_ix6, 1)
            e.wait_ge(s_srt, G)
            over_groups(e, copy_indices)

            e.wait_ge(s_wT, 1)
            for h in range(2):
                last = nc.scalar.activation(wT[h * D:(h + 1) * D, h, :], bank[3][h * D:(h + 1) * D, 0:D],
                                            ACT.Copy)
            last.then_inc(s_wTs, 1)
            e.sem_inc(s_hTs, 2)
            def h2_copies(i, j, q):
                e.wait_ge(s_hT, pair_through(j))
                e.wait_ge(s_lin, pair_through(j - 2))
                nc.scalar.activation(eaT[:, q, :], bank[0][:, q * P:(q + 1) * P],
                                     ACT.Copy).then_inc(s_hTs, 1)
            over(e, NP, h2_copies)
            deviation(3)

        @block.tensor
        def _(e):
            regs2, regs5, regs6 = ([e.alloc_register(f"pe_{name}{n}") for name in ("seen", "free")]
                                   for n in (2, 5, 6))
            seen4 = e.alloc_register("pe_seen4")
            for r in (regs2[0], regs5[0], regs6[0], seen4):
                e.reg_mov(r, 0)
            for s_of, n in ((s_xT, 2), (s_n1, 2), (s_n2, 2), (s_tp, BIAS), (s_l1, BIAS), (s_l2, BIAS),
                            (s_hist, BIAS), (s_pa, BIAS), (s_free5, 2), (s_free6, 2), (s_hT, 2), (s_lin, 2)):
                e.sem_inc(s_of, n)
            for s in range(S):
                e.sem_inc(s_u4[s], 1)
            e.wait_ge(s_const, 1)
            e.wait_ge(s_load, 16 * N_LOADS)

            def node_network(i, j, q):
                e.wait_ge(s_xr[q], (i + 1) * 16 if not (isinstance(j, int) and j == NP - 1) else (i + 2) * 16)
                e.wait_ge(s_xTs, pair_through(j - 2))
                nc.tensor.transpose(bank[0][:, q * P:(q + 1) * P],
                                    ea[:, q, 0:4, :].rearrange("p k f -> p (k f)"), ident[:, :])\
                    .then_inc(s_xT, 1)
                e.wait_ge(s_xTs, pair_through(j))
                e.wait_ge(s_nb, pair_through(j - 2))
                for h in range(2):
                    mm = nc.tensor.matmul(bank[1 + q][:, h * P:(h + 1) * P], w1n[:, h, :],
                                          eaT[:, q, :], start=True, stop=True)
                mm.then_inc(s_n1, 1)
                e.wait_ge(s_nl, pair_through(j))
                e.wait_ge(s_nc, pair_through(j - 2))
                for h in range(2):
                    o = bank[3 + q][:, h * D:(h + 1) * D]
                    nc.tensor.matmul(o, ones_f[:, :], b2n_r[:, :], start=True, stop=False)
                    mm = nc.tensor.matmul(o, hl[:, q, h * P:(h + 1) * P], w2n[:, :], start=False, stop=True)
                mm.then_inc(s_n2, 1)
            over(e, NP, node_network)

            e.wait_ge(s_rngld[0], 16)
            open_sums(e, v2, D + 1)
            nc.tensor.matmul(bank[5][0:B, 0:1], ones_b[0:1, 0:B], zeros_b[:, 0:1], start=True, stop=False)
            def transpose(g, q, s):
                w = W_OF[s] * DE
                e.wait_ge(s_tc, through(step(g, s) - 1))
                nc.tensor.transpose(bank[0][0:w, 0:P],
                                    ea[:, q, tiles(s), :].rearrange("p k f -> p (k f)"), ident[:, :])\
                    .then_inc(s_tp, 1)

            def layer1(g, s):
                e.wait_ge(s_tc, through(step(g, s)))
                e.wait_ge(s_eb, through(before(g, s)))
                o = hidden(s)
                if W_OF[s] == Q:
                    for h in range(2):
                        mm = nc.tensor.matmul(o[:, h * P:(h + 1) * P], w1e[:, h, :], eaT[:, s % 4, :],
                                              start=True, stop=True)
                else:
                    mm = nc.tensor.matmul(o[0:D, 0:P], w1e[0:DE, 0, 0:D], eaT[0:DE, s % 4, :],
                                          start=True, stop=True)
                mm.then_inc(s_l1, 1)

            def layer2(g, s):
                w = W_OF[s]
                e.wait_ge(s_lk, through(step(g, s)))
                e.wait_ge(s_msg, through(before(g, s)))
                o = edge_out(s)
                nc.tensor.matmul(o[:, 0:w * D], ones_b[0:3, :],
                                 b2e_3[:, :].unsqueeze(1).to_broadcast([3, w, D]), start=True, stop=False)
                if w == Q:
                    for h in range(2):
                        mm = nc.tensor.matmul(o[:, h * P:(h + 1) * P], hl[:, s % 4, h * P:(h + 1) * P],
                                              w2e[:, :, :].rearrange("p t f -> p (t f)"),
                                              start=False, stop=(h == 1))
                else:
                    mm = nc.tensor.matmul(o[:, 0:D], hl[0:D, s % 4, 0:P], w2e[0:D, 0, :],
                                          start=False, stop=True)
                mm.then_inc(s_l2, 1)

            e.wait_ge(s_b3, 1)
            e.wait_ge(s_ea[0], 16)
            transpose(0, 0, 0)
            transpose(0, 0, 1)
            layer1(0, 0)
            transpose(0, 0, 2)
            layer1(0, 1)
            def edge_network(i, g, q):
                for s in range(S):
                    if (t := ahead(g, q, s + 3)) is not None:
                        if t[2] == 0:
                            e.wait_ge(s_ea[1 - q], (i + 1 + q) * 16)
                        transpose(*t)
                    if (t := ahead(g, q, s + 2)) is not None:
                        layer1(t[0], t[2])
                    layer2(g, s)
                    e.wait_ge(s_ob, through(step(g, s)))
                    for k in range(W_OF[s]):
                        mm = nc.tensor.matmul(bank[5][0:B, 0:1], ob[:, s % 2, k, :], ones_b[:, 0:1],
                                              start=False, stop=False)
                    mm.then_inc(s_hist, 1)
                sum_by_node(e, v2, regs2, g, q, 0, msg[:, q, :, 0:D + 1])
            over_groups(e, edge_network)
            nc.tensor.matmul(bank[5][0:B, 0:1], ones_b[0:1, 0:B], zeros_b[:, 0:1], start=False, stop=True)\
                .then_inc(s_total, 1)

            e.wait_ge(s_cT, 1)
            nc.tensor.matmul(bank[4][:, 0:B], counts_T[0:B, :], upper_f[0:B, 0:B], start=True, stop=True)\
                .then_inc(s_bases, 1)

            e.wait_ge(s_g1, 1)
            def select_rows(i, g, q):
                e.wait_ge(s_rec, g + 1)
                for c in range(4):
                    nc.tensor.matmul(bank[c][:, :], ones_b[0:1, :], zeros_b[:, :], start=True, stop=False)
                lo, hi = block_range(e, g, 0)
                with e.Fori(lo, hi + 1) as blk:
                    n = e.snap(seen4)
                    blk = a_block(blk)
                    for s in range(S):
                        e.wait_ge(s_m4[s], n + 1)
                        for k in range(Q * s, Q * s + W_OF[s]):
                            mm = nc.tensor.matmul(bank[k // 8][:, (k % 8) * D:(k % 8 + 1) * D], OH[:, k, :],
                                                  U[:, bass.ds(blk, 1), :].rearrange("p a f -> p (a f)"),
                                                  start=False, stop=False)
                        mm.then_inc(s_u4[s], 1)
                    e.reg_add(seen4, seen4, 1)
                for c in range(4):
                    mm = nc.tensor.matmul(bank[c][:, :], ones_b[0:1, :], zeros_b[:, :], start=False, stop=True)
                mm.then_inc(s_sel, 1)

                for s in range(S):
                    w = W_OF[s]
                    rank = bank[4 + s % 2][:, 0:(Q + 1) * B].rearrange("p (k b) -> p k b", b=B)
                    e.wait_ge(s_ob4, through(step(g, s)))
                    e.wait_ge(s_pl, through(before(g, s)))
                    nc.tensor.matmul(rank[:, 0:w + 1, :], ones_b[0:1, :], zeros_b[:, 0:(w + 1) * B],
                                     start=True, stop=False)
                    for k in range(w):
                        nc.tensor.matmul(rank[:, k, :], upper[:, :], ob[:, s % 3, k, :],
                                         start=False, stop=False)
                        n = w - k
                        mm = nc.tensor.matmul(rank[:, k + 1:w + 1, :], ones_b[:, :],
                                              ob[:, s % 3, k:k + 1, :].to_broadcast([P, n, B]),
                                              start=False, stop=(k == w - 1))
                    mm.then_inc(s_pa, 1)
            over_groups(e, select_rows)

            e.wait_ge(s_rngld[1], 16)
            open_sums(e, v5, D)
            def sum_sorted(i, g, q):
                sum_by_node(e, v5, regs5, g, q, 1, msg[:, q, :, 0:D])
                group_summed(s_free5)
            over_groups(e, sum_sorted)
            e.wait_ge(s_g2, 1)
            open_sums(e, v6, D)
            def sum_hop(i, g, q):
                e.wait_ge(s_rows6[q], (i + 1) * (16 * K))
                sum_by_node(e, v6, regs6, g, q, 1, rows[:, q, :, :])
                group_summed(s_free6)
            over_groups(e, sum_hop)

            nc.tensor.transpose(bank[3][:, 0:D], w_sb[:, :, :].rearrange("p a f -> p (a f)"),
                                ident[0:D, 0:D]).then_inc(s_wT, 1)
            e.wait_ge(s_wTs, 1)
            def last_product(i, j, q):
                e.wait_ge(s_h2, pair_through(j))
                e.wait_ge(s_hTs, pair_through(j - 2))
                nc.tensor.transpose(bank[0][:, q * P:(q + 1) * P],
                                    hb[:, q, 0:P], ident[:, :]).then_inc(s_hT, 1)
                e.wait_ge(s_hTs, pair_through(j))
                e.wait_ge(s_res, pair_through(j - 2))
                for h in range(2):
                    o = bank[1 + q][:, h * D:(h + 1) * D]
                    nc.tensor.matmul(o, ones_f[:, :], b_r[:, :], start=True, stop=False)
                    mm = nc.tensor.matmul(o, eaT[:, q, :], wT[:, h, :],
                                          start=False, stop=True)
                mm.then_inc(s_lin, 1)
            over(e, NP, last_product)

        @block.vector
        def _(e):
            done = [0]

            def link(ins):
                done[0] += 1
                ins.then_inc(s_dv, 1)
                e.wait_ge(s_dv, done[0])

            regs2, regs5, regs6 = ([e.alloc_register(f"dve_{name}{n}") for name in ("seen", "blk", "row")]
                                   for n in (2, 5, 6))
            seen4 = e.alloc_register("dve_seen4")
            for r in (*regs2[:2], *regs5[:2], *regs6[:2], seen4):
                e.reg_mov(r, 0)
            for r in (regs2[2], regs5[2], regs6[2]):
                e.reg_mov(r, 1)

            def pack_ranges(low_high):
                link(nc.vector.scalar_tensor_tensor(
                    out=rng_f[0:G, 0:1], in0=low_high[0:G, 1:2], scalar=256.0, in1=low_high[0:G, 0:1],
                    op0=ALU.mult, op1=ALU.add))
                nc.vector.tensor_copy(rng_i[0:G, 0:1], rng_f[0:G, 0:1]).then_inc(s_rngd, 1)

            for s_of, n in ((s_nl, 2), (s_nc, 2), (s_lk, BIAS), (s_msg, BIAS), (s_ob, BIAS), (s_ob4, BIAS),
                            (s_pl, BIAS), (s_run, BIAS), (s_pm, BIAS), (s_pr, BIAS), (s_pi, 2),
                            (s_h2, 2), (s_res, 2)):
                e.sem_inc(s_of, n)
            for v in (v2, v5, v6):
                e.sem_inc(v.added, 1)
            nc.vector.memset(w1e[:, :, :], 0.0)
            nc.vector.memset(w2e[:, :, :], 0.0)
            nc.vector.memset(w1n[:, :, :], 0.0)
            nc.vector.memset(wT[:, :, :], 0.0)
            nc.vector.memset(X[:, B - 1, :], 0.0)
            nc.vector.memset(ea[:, :, :, :], 0.0).then_inc(s_wzero, 1)

            e.wait_ge(s_dg, 16)
            link(nc.vector.tensor_reduce(rng_f[0:G, 0:1], dst_g[0:G, :], AX.X, ALU.min))
            link(nc.vector.tensor_reduce(rng_f[0:G, 1:2], dst_g[0:G, :], AX.X, ALU.max))
            link(nc.vector.tensor_copy(rng_i[0:G, :], rng_f[0:G, :]))
            link(nc.vector.tensor_scalar(rng_i[0:G, :], rng_i[0:G, :], 7, None, ALU.arith_shift_right))
            pack_ranges(rng_i)
            link(nc.vector.memset(tab[:, :], 0.0))

            def node_values(i, j, q):
                e.wait_ge(s_nb, pair_through(j))
                e.wait_ge(s_n2, pair_through(j - 2))
                nc.vector.scalar_tensor_tensor(out=hl[:, q, :], in0=hb[:, q, :], scalar=SLOPE,
                                               in1=hb[:, q, :], op0=ALU.mult, op1=ALU.max).then_inc(s_nl, 1)
                e.wait_ge(s_n2, pair_through(j))
                nc.vector.tensor_copy(U[:, bass.ds(j * 2, 2), :],
                                      bank[3 + q][:, 0:2 * D].rearrange("p (b f) -> p b f", f=D))\
                    .then_inc(s_nc, 1)
            over(e, NP, node_values)

            e.wait_ge(s_load, 16 * N_LOADS)
            e.wait_ge(s_const, 1)
            for part in range(3):
                link(nc.vector.tensor_copy(b2e_p[:, part, :], b2e_f[:, :]))
                link(nc.vector.tensor_tensor(b2e_f[:, :], b2e_f[:, :], b2e_p[:, part, :], ALU.subtract))
            link(nc.vector.tensor_scalar(b2e_3[:, :], b2e_p[:, 0, :], ident[0:3, 0:1], None, ALU.mult))
            for part in range(1, 3):
                link(nc.vector.scalar_tensor_tensor(
                    out=b2e_3[:, :], in0=b2e_p[:, part, :], scalar=ident[0:3, part:part + 1],
                    in1=b2e_3[:, :], op0=ALU.mult, op1=ALU.add))
            e.sem_inc(s_b3, 1)
            e.wait_ge(s_ids, 32)
            e.wait_ge(s_rngld[0], 16)

            def mark_buckets(s, q, signal, depth=2):
                w = W_OF[s]
                nc.vector.tensor_tensor(ob[:, s % depth, 0:w, :],
                                        bucket[:, q, tiles(s)].unsqueeze(2).to_broadcast([P, w, B]),
                                        iota_n[:, 0:B].unsqueeze(1).to_broadcast([P, w, B]),
                                        ALU.is_equal).then_inc(signal, 1)

            def leaky(g, s):
                parts, cols = (P, 2 * P) if W_OF[s] == Q else (D, P)
                e.wait_ge(s_eb, through(step(g, s)))
                e.wait_ge(s_l2, through(before4(g, s)))
                nc.vector.scalar_tensor_tensor(
                    out=hl[0:parts, s % 4, 0:cols], in0=hb[0:parts, s % 4, 0:cols], scalar=SLOPE,
                    in1=hb[0:parts, s % 4, 0:cols], op0=ALU.mult, op1=ALU.max).then_inc(s_lk, 1)

            leaky(0, 0)
            def messages(i, g, q):
                def message(s):
                    w = W_OF[s]
                    e.wait_ge(s_l2, through(step(g, s)))
                    e.wait_ge(s_rows[q][s], (i + 1) * (16 * w))
                    nc.vector.tensor_tensor(msg[:, q, tiles(s), 0:D],
                                            edge_out(s)[:, 0:w * D].rearrange("p (k f) -> p k f", f=D),
                                            rows[:, q, tiles(s), :], ALU.mult).then_inc(s_msg, 1)

                nc.vector.tensor_scalar(bucket[:, q, :], src_cols(g), 7, None,
                                        ALU.arith_shift_right).then_inc(s_bk, 1)
                e.wait_ge(s_bk, g + 1)
                for s in range(S):
                    if (t := ahead(g, q, s + 1)) is not None:
                        leaky(t[0], t[2])
                    e.wait_ge(s_hist, through(before(g, s)))
                    mark_buckets(s, q, s_ob)
                    if s > 0:
                        message(s - 1)
                message(S - 1)
                mark_and_add(e, v2, regs2, g, q, 0, dst_flat, tab, D + 1)
            over_groups(e, messages)

            add_last(e, v2, e.snap(regs2[0]), regs2[1], regs2[2], tab, D + 1)
            e.wait_ge(v2.added, e.snap(regs2[0]) + 2)
            wide = [P, B, D]

            def spread(t):
                return t.unsqueeze(2).to_broadcast(wide)

            def norm(t, to, squares, n):
                link(nc.vector.tensor_reduce(mean[:, :], t, AX.X, ALU.add))
                link(nc.vector.tensor_scalar(mean[:, :], mean[:, :], 1.0 / D, None, ALU.mult))
                link(nc.vector.tensor_tensor(t, t, spread(mean[:, :]), ALU.subtract))
                link(nc.vector.tensor_tensor(squares, t, t, ALU.mult))
                link(nc.vector.tensor_reduce(var[:, :], squares, AX.X, ALU.add))
                nc.vector.tensor_scalar(var[:, :], var[:, :], 1.0 / D, EPS, ALU.mult, ALU.add)\
                    .then_inc(s_var, 1)
                e.wait_ge(s_dev, n + 1)
                link(nc.vector.reciprocal(std[:, :], std[:, :]))
                link(nc.vector.tensor_tensor(to, t, spread(std[:, :]), ALU.mult))

            e.wait_ge(s_load, 16 * N_LOADS)
            e.wait_ge(s_xld, 32)
            e.wait_ge(s_nst, 16)
            nc.vector.tensor_scalar(var[:, :], agg0[:, :, D], 1.0, None, ALU.add).then_inc(s_var, 1)
            link(nc.vector.tensor_tensor(scale[:, :], scl[:, 0:1], scl[:, 1:2], ALU.mult))
            link(nc.vector.scalar_tensor_tensor(out=U[:, :, :], in0=agg0[:, :, 0:D], scalar=scale[:, 0:1],
                                                in1=X[:, :, :], op0=ALU.mult, op1=ALU.add))
            e.wait_ge(s_dev, 1)
            link(nc.vector.reciprocal(dinv[:, :], std[:, :]))
            norm(U[:, :, :], U[:, :, :], H[:, :, :], 1)
            link(nc.vector.tensor_tensor(U[:, :, :], U[:, :, :], gam[:, :].unsqueeze(1).to_broadcast(wide), ALU.mult))
            link(nc.vector.tensor_tensor(U[:, :, :], U[:, :, :], bet[:, :].unsqueeze(1).to_broadcast(wide), ALU.add))
            link(nc.vector.tensor_tensor(U[:, :, :], U[:, :, :], X[:, :, :], ALU.add))
            norm(U[:, :, :], X[:, :, :], H[:, :, :], 2)
            nc.vector.tensor_tensor(U[:, :, :], X[:, :, :], spread(dinv[:, :]), ALU.mult)
            nc.vector.memset(H_all[:, :, :], 0.0)
            e.wait_ge(s_total, 1)
            nc.vector.tensor_copy(counts_T[0:B, :], bank[5][0:B, 0:1].to_broadcast([B, P])).then_inc(s_cT, 1)
            e.wait_ge(s_bases, 1)
            link(nc.vector.tensor_copy(place[:, 0, :], bank[4][:, 0:B]))
            for a in range(2):
                link(nc.vector.tensor_scalar(cmp_w[0:G, a, 0:B - 1], place[0:G, 0, 1:B], thr[0:G, a:a + 1],
                                             None, ALU.is_le))
            link(nc.vector.tensor_reduce(rng_f[0:G, :], cmp_w[0:G, :, 0:B - 1], AX.X, ALU.add))
            pack_ranges(rng_f)
            e.sem_inc(s_g1, 1)

            def marks_and_places(i, g, q):
                e.wait_ge(s_row[q], (i + 1) * 16)
                by_tile = dst_row[:, q, :].rearrange("p (e k) -> p k e", k=K)
                lo, hi = block_range(e, g, 0)
                with e.Fori(lo, hi + 1) as blk:
                    n = e.snap(seen4)
                    blk = a_block(blk)
                    for s in range(S):
                        e.wait_ge(s_u4[s], n + 1)
                        nc.vector.tensor_scalar(OH[:, tiles(s), :], by_tile[:, tiles(s), :],
                                                node_id[:, bass.ds(blk, 1)], None,
                                                ALU.is_equal).then_inc(s_m4[s], 1)
                    e.reg_add(seen4, seen4, 1)

                nc.vector.tensor_scalar(bucket[:, q, :], src_cols(g), 7, None,
                                        ALU.arith_shift_right).then_inc(s_bk4, 1)
                e.wait_ge(s_bk4, g + 1)
                e.wait_ge(s_pr, through(step(g, 0) - 1))
                mark_buckets(0, q, s_ob4, 3)

                def add_places(s):
                    w = W_OF[s]
                    rank = bank[4 + s % 2][:, 0:(Q + 1) * B].rearrange("p (k b) -> p k b", b=B)
                    now, after = place[:, (q + s) % 2, :], place[:, (q + s + 1) % 2, :]
                    e.wait_ge(s_pa, through(step(g, s)))
                    e.wait_ge(s_run, through(step(g, s) - 1))
                    e.wait_ge(s_pl, through(step(g, s) - 1))
                    nc.vector.tensor_tensor(after, now, rank[:, w, :], ALU.add).then_inc(s_run, 1)
                    e.wait_ge(s_pr, through(step(g, s) - 3))
                    nc.vector.tensor_tensor(rank_w[:, s % 3, 0:w, :], rank[:, 0:w, :],
                                            now.unsqueeze(1).to_broadcast([P, w, B]),
                                            ALU.add).then_inc(s_pl, 1)

                def pick_place(s):
                    r = rank_w[:, s % 3, 0:W_OF[s], :]
                    e.wait_ge(s_pl, through(step(g, s)))
                    nc.vector.tensor_tensor(r, r, ob[:, s % 3, 0:W_OF[s], :], ALU.mult).then_inc(s_pm, 1)

                def sum_place(s):
                    e.wait_ge(s_pm, through(step(g, s)))
                    nc.vector.tensor_reduce(pos_f[:, q, tiles(s)], rank_w[:, s % 3, 0:W_OF[s], :], AX.X,
                                            ALU.add).then_inc(s_pr, 1)

                for s in range(S + 2):
                    if s < S:
                        add_places(s)
                    if s + 1 < S:
                        if s + 1 >= 3:
                            e.wait_ge(s_pm, through(step(g, s + 1) - 3))
                        mark_buckets(s + 1, q, s_ob4, 3)
                    if 1 <= s <= S:
                        pick_place(s - 1)
                    if s >= 2:
                        sum_place(s - 2)
                e.wait_ge(s_pr, through(step(g, S - 1)))
                e.wait_ge(s_rec, g + 2)
                nc.vector.tensor_copy(pos_i[:, q, :], pos_f[:, q, :]).then_inc(s_pi, 1)
            over_groups(e, marks_and_places)

            e.wait_ge(s_rngld[1], 16)
            def keep_and_mark(i, g, q):
                e.wait_ge(s_m[q], (i + 1) * 16)
                nc.vector.tensor_copy(src_cols(g).unsqueeze(2), msg[:, q, :, D:D + 1].bitcast(i32))
                nc.vector.tensor_copy(dst_cols(g).unsqueeze(2), msg[:, q, :, D + 1:R].bitcast(i32))\
                    .then_inc(s_srt, 1)
                e.wait_ge(s_srt, g + 1)
                mark_and_add(e, v5, regs5, g, q, 1, src_flat, H_flat, D)
            over_groups(e, keep_and_mark)
            add_last(e, v5, e.snap(regs5[0]), regs5[1], regs5[2], H_flat, D)
            e.wait_ge(v5.added, e.snap(regs5[0]) + 2)
            link(nc.vector.tensor_tensor(H[:, :, :], H[:, :, :], U[:, :, :], ALU.add))
            link(nc.vector.tensor_tensor(H[:, :, :], H[:, :, :], spread(dinv[:, :]), ALU.mult))
            link(nc.vector.tensor_tensor(U[:, :, :], H[:, :, :], spread(dinv[:, :]), ALU.mult))
            nc.vector.memset(H_all[:, :, :], 0.0).then_inc(s_g2, 1)

            def mark_hop(i, g, q):
                mark_and_add(e, v6, regs6, g, q, 1, src_flat, H_flat, D)
            over_groups(e, mark_hop)
            add_last(e, v6, e.snap(regs6[0]), regs6[1], regs6[2], H_flat, D)
            e.wait_ge(v6.added, e.snap(regs6[0]) + 2)
            e.sem_inc(s_turn["vector"], 1)

            def h2_and_residual(i, j, q):
                pair = bass.ds(j * 2, 2)
                h2 = hb[:, q, 0:P].rearrange("p (b f) -> p b f", f=D)
                e.wait_ge(s_hT, pair_through(j - 2))
                nc.vector.tensor_tensor(h2, H[:, pair, :], U[:, pair, :], ALU.add).then_inc(s_ha, 1)
                e.wait_ge(s_ha, j + 1)
                nc.vector.tensor_tensor(h2, h2, dinv[:, pair].unsqueeze(2).to_broadcast([P, 2, D]),
                                        ALU.mult).then_inc(s_h2, 1)
                e.wait_ge(s_lin, pair_through(j))
                nc.vector.tensor_tensor(H[:, pair, :], X[:, pair, :],
                                        bank[1 + q][:, 0:P].rearrange("p (b f) -> p b f", f=D),
                                        ALU.add).then_inc(s_res, 1)
            over(e, NP, h2_and_residual)
            e.wait_ge(s_res, pair_through(NP - 1))
            norm(H[:, :, :], H[:, :, :], U[:, :, :], 3)
            e.sem_inc(s_fin, 1)


_INS = ['x', 'src', 'dst', 'edge_attr_32', 'L0_gnn_W1n', 'L0_gnn_b1n', 'L0_gnn_W2n', 'L0_gnn_b2n',
        'L0_gnn_W1e', 'L0_gnn_b1e', 'L0_gnn_W2e', 'L0_gnn_b2e', 'L0_gnn_res_w', 'L0_gnn_dp_scale',
        'L0_gnn_gamma', 'L0_gnn_beta', 'L1_gnn_W', 'L1_gnn_b']


def kernel(**inputs):
    import numpy as np
    import concourse.bacc as bacc
    from concourse.bass_utils import run_bass_kernel_spmd

    nc = bacc.Bacc("TRN2", target_bir_lowering=False, num_devices=1)
    arrays, args = {}, []
    for name in _INS:
        a = np.ascontiguousarray(inputs[name])
        arrays[f"in_{name}"] = a
        args.append(nc.dram_tensor(f"in_{name}", a.shape, mybir.dt.from_np(a.dtype), kind="ExternalInput").ap())
    out = nc.dram_tensor("out", inputs["x"].shape, mybir.dt.float32, kind="ExternalOutput").ap()
    gnn_two_layers(nc, *args, out)
    r = run_bass_kernel_spmd(nc, [arrays], core_ids=[0])
    return r.results[0]["out"]
```

```python
import concourse.bass as bass
from concourse import mybir
from contextlib import ExitStack


def gnn_two_layers(nc, x, src, dst, edge_attr, W1n, b1n, W2n, b2n, W1e, b1e, W2e, b2e,
                   res_w, dp_scale, gamma, beta, W, b, out):
    f32, i32, bf16 = mybir.dt.float32, mybir.dt.int32, mybir.dt.bfloat16
    ALU, ACT, AX = mybir.AluOpType, mybir.ActivationFunctionType, mybir.AxisListType

    P = 128
    N, D = x.shape
    E, DE = edge_attr.shape
    HN = W1n.shape[1]
    EPS = 1e-5
    SLOPE = 0.1
    K = 25
    GE = K * P
    G = E // GE
    assert G * GE == E and HN == P and D == 64 and DE == 32
    B = -(-N // P)
    NL = N - (B - 1) * P
    IDS = 3 * D // 2
    R = IDS + 2
    PW = D + 2
    Q = 4
    S = -(-K // Q)
    W_OF = [min(Q, K - Q * s) for s in range(S)]
    BIAS = 2 * S
    BP = B
    NP = B // 2
    assert B % 2 == 0 and NP % 2 == 1
    assert B * Q <= 512 and S == 7 and G % 2 == 1 and B < 128

    ctx = ExitStack()
    with ctx:
        def sb(name, shape, dt=f32):
            return ctx.enter_context(nc.sbuf_tensor(name, shape, dt))

        def sem(name):
            return ctx.enter_context(nc.semaphore(name))

        node_rows = nc.dram_tensor("node_rows", [BP * P, D], f32).ap()
        hop_rows = nc.dram_tensor("hop_rows", [BP * P, D], f32).ap()
        sorted_rows = nc.dram_tensor("sorted_rows", [E, R], f32).ap()
        range_dram = nc.dram_tensor("range_dram", [2, P], i32).ap()

        X = sb("X", [P, BP, D])
        PARTS_W = 2 * K * 3 * PW // 2
        TAB_W = max((B + 1) * (D + 1), 2 * GE)
        tab = sb("tab", [P, max(TAB_W, PARTS_W)])
        agg0 = tab[:, 0:B * (D + 1)].rearrange("p (b f) -> p b f", f=D + 1)
        dst_row = tab[:, 0:2 * GE].bitcast(i32).rearrange("p (q e) -> p q e", q=2)
        U = sb("U", [P, BP, D])
        H_all = sb("H", [P, max(B + 1, -(-PARTS_W // D)), D])
        H = H_all[:, 0:B, :]
        src_i = sb("src_i", [P, G, K], i32)
        dst_i = sb("dst_i", [P, G, K], i32)
        work = sb("work", [P, max(2 * K * (D + DE), 2 * K * R)])
        msg = work[:, 0:2 * K * D].rearrange("p (q k f) -> p q k f", q=2, k=K)
        ea = work[:, 2 * K * D:2 * K * (D + DE)].rearrange("p (q k f) -> p q k f", q=2, k=K)
        rec = work[:, 0:2 * K * R].rearrange("p (q k r) -> p q k r", q=2, k=K)
        rec_bf16 = work[:, 0:2 * K * R].bitcast(bf16).rearrange("p (q k r) -> p q k r", q=2, k=K)
        eaT = sb("eaT", [P, 4, P])
        hidden_v = sb("hidden_v", [P, 16 * P])
        hb = hidden_v[:, 0:8 * P].rearrange("p (a e) -> p a e", a=4)
        hl = hidden_v[:, 8 * P:16 * P].rearrange("p (a e) -> p a e", a=4)
        rest4 = hidden_v[:, 0:K * D].rearrange("p (k f) -> p k f", k=K)
        rows = sb("rows", [P, 2, K, D])
        OH = sb("OH", [P, K, 2 * P], bf16)
        ob = sb("ob", [P, 3, Q, B], bf16)
        rank_w = sb("rank_w", [P, 3, Q, B])
        idx = sb("idx", [P, 2, K], i32)
        bucket = sb("bucket", [P, 2, K], i32)
        pos_f = sb("pos_f", [P, 2, K])
        pos_i = sb("pos_i", [P, 2, K], i32)
        iota_n = sb("iota_n", [P, P])
        iota_2 = sb("iota_2", [P, 2 * P], bf16)
        local = sb("local", [P, 2, K])
        block0 = sb("block0", [P, B + 1])
        node_id = sb("node_id", [P, BP])
        ident = sb("ident", [P, P])
        upper = sb("upper", [P, P], bf16)
        upper_f = sb("upper_f", [P, P])
        counts_T = sb("counts_T", [P, P])
        ones_b = sb("ones_b", [P, P], bf16)
        zeros_b = sb("zeros_b", [1, 512], bf16)
        assert (Q + 1) * B <= 512
        ones_f = sb("ones_f", [1, P])
        w1n = sb("w1n", [P, 2, P])
        w2n = sb("w2n", [P, D])
        b1n_c = sb("b1n_c", [P, 1])
        b2n_r = sb("b2n_r", [1, D])
        w1e = sb("w1e", [P, 2, P])
        w2e = sb("w2e", [P, 2, D])
        b1e_c = sb("b1e_c", [P, 1])
        b2e_f = sb("b2e_f", [3, D])
        b2e_p = sb("b2e_p", [3, 3, D], bf16)
        b2e_3 = sb("b2e_3", [3, D], bf16)
        w_sb = sb("w_sb", [D, 2, D])
        wT = sb("wT", [P, 2, D])
        b_r = sb("b_r", [1, D])
        gam = sb("gam", [P, D])
        bet = sb("bet", [P, D])
        scl = sb("scl", [P, 2])
        scale = sb("scale", [P, 1])
        mean = sb("mean", [P, BP])
        var = sb("var", [P, BP])
        std = sb("std", [P, BP])
        dinv = sb("dinv", [P, BP])
        place = sb("place", [P, 2, B])
        thr = sb("thr", [P, 2])
        cmp_w = sb("cmp_w", [P, 2, B])
        rng_f = sb("rng_f", [P, 2])
        rng_i = sb("rng_i", [P, 2], i32)
        dst_g = OH[:, :, :].rearrange("p k e -> p (k e)").bitcast(i32)
        OH4 = OH[:, :, 0:P]
        parts_2 = H_all[:, :, :].rearrange("p b f -> p (b f)")[:, 0:PARTS_W].bitcast(bf16)\
            .rearrange("p (q k t f) -> p q k t f", q=2, k=K, t=3)
        parts_6 = tab[:, 0:PARTS_W].bitcast(bf16).rearrange("p (q k t f) -> p q k t f", q=2, k=K, t=3)
        g1_hi = rows[:, :, :, :].rearrange("p q k f -> p (q k f)")[:, 0:B * D // 2].bitcast(bf16)\
            .rearrange("p (b f) -> p b f", f=D)
        g1_low = H_all[:, :, :].rearrange("p b f -> p (b f)")[:, 0:B * D].bitcast(bf16)\
            .rearrange("p (t b f) -> p t b f", t=2, f=D)
        g1_parts = [g1_hi, g1_low[:, 0], g1_low[:, 1]]
        rng_d = sb("rng_d", [1, 2, P], i32)

        bank = [ctx.enter_context(nc.psum_tensor(f"bank{i}", [P, 512], f32)) for i in range(6)]
        sums = ctx.enter_context(nc.psum_tensor("sums", [P, 2, 512], f32))

        s_turn = {k: sem(f"{k}_turns") for k in ("sync", "gpsimd", "vector")}
        s_fill = sem("fills_landed")
        s_const = sem("constants_made")
        s_wzero = sem("weight_tiles_zeroed")
        s_load = sem("weights_loaded")
        s_xld = sem("x_loaded")
        s_ids = sem("indices_loaded")
        s_dg = sem("dst_groups_loaded")
        s_dv = sem("vector_op_done")
        s_rngd = sem("ranges_made")
        s_rngst = sem("ranges_stored")
        s_rngld = [sem("dst_ranges_loaded"), sem("src_ranges_loaded")]
        s_xr = [sem(f"x_pair_in{q}") for q in range(2)]
        s_xT = sem("x_transposed")
        s_xTs = sem("x_transpose_copied")
        s_n1 = sem("node_layer1_done")
        s_nb = sem("node_bias_done")
        s_nl = sem("node_leaky_done")
        s_n2 = sem("node_layer2_done")
        s_nc = sem("node_rows_copied")
        s_nst = sem("node_rows_stored")
        s_ea = [sem(f"edge_features_in{q}") for q in range(2)]
        s_idx = [sem(f"src_indices_in{q}") for q in range(2)]
        s_ix6 = [sem(f"dst_indices_in{q}") for q in range(2)]
        s_tp = sem("edge_transposed")
        s_tc = sem("edge_transpose_copied")
        s_l1 = sem("edge_layer1_done")
        s_eb = sem("edge_bias_done")
        s_lk = sem("edge_leaky_done")
        s_l2 = sem("edge_layer2_done")
        s_b3 = sem("edge_bias_parts_made")
        s_msg = sem("messages_made")
        s_bk = sem("bucket_ids_made")
        s_ob = sem("buckets_marked")
        s_hist = sem("buckets_counted")
        s_total = sem("bucket_totals_ready")
        s_rows = [[sem(f"rows_gathered{q}_{s}") for s in range(S)] for q in range(2)]
        s_var = sem("variance_made")
        s_dev = sem("deviation_made")
        s_cT = sem("counts_spread")
        s_bases = sem("bases_summed")
        s_g1 = sem("stage3_done")
        s_row = [sem(f"dst_row_in{q}") for q in range(2)]
        s_m4 = [sem(f"node_marks{i}") for i in range(S)]
        s_u4 = [sem(f"node_marks_used{i}") for i in range(S)]
        s_sel = sem("group_rows_selected")
        s_bk4 = sem("bucket_ids_made_again")
        s_ob4 = sem("buckets_marked_again")
        s_pa = sem("ranks_ready")
        s_pl = sem("places_of_blocks_added")
        s_run = sem("next_places_advanced")
        s_pm = sem("ranks_picked")
        s_pr = sem("positions_summed")
        s_pi = sem("positions_rounded")
        s_sc = [sem(f"rows_scattered{q}") for q in range(2)]
        s_m = [sem(f"sorted_rows_in{q}") for q in range(2)]
        s_srt = sem("sorted_ids_kept")
        s_zero = sem("sums_zeroed")
        s_g2 = sem("hop_rows_made")
        s_g2st = sem("hop_rows_stored")
        s_rows6 = [sem(f"hop_rows_gathered{q}") for q in range(2)]
        s_wT = sem("W_transposed")
        s_wTs = sem("W_transpose_copied")
        s_ha = sem("hop_sum_with_loop")
        s_h2 = sem("h2_made")
        s_hT = sem("h2_transposed")
        s_hTs = sem("h2_transpose_copied")
        s_lin = sem("last_product_done")
        s_res = sem("residual_added")
        s_fin = sem("output_made")
        s_out = sem("output_stored")

        class Visits:

            def __init__(self, tag):
                self.high = sem(f"{tag}_high_parts_made")
                self.rest1 = sem(f"{tag}_first_rest_made")
                self.mid = sem(f"{tag}_middle_parts_made")
                self.rest2 = sem(f"{tag}_second_rest_made")
                self.low = sem(f"{tag}_low_parts_made")
                self.done = sem(f"{tag}_group_summed")

        s_local = sem("visit_local_ids_made")
        s_marks = [sem(f"visit_marks{s}") for s in range(S)]
        s_used = [sem(f"visit_marks_used{s}") for s in range(S)]
        s_added = sem("visit_added")
        v2, v4, v6 = Visits("message"), Visits("hop1"), Visits("hop2")

        block = ctx.enter_context(nc.Block())

        def step(g, s):
            return g * S + s

        def through(n):
            return n + (1 + BIAS)

        def before(g, s):
            return step(g, s) - (1 if s == 0 else 2)

        def before4(g, s):
            return step(g, s) - (4 if s >= 4 else 7 if s == 3 else 3)

        def hidden(s):
            return bank[1 + s % 2]

        def edge_out(s):
            return bank[3 + s % 2]

        def ahead(g, q, s):
            if s < S:
                return g, q, s
            return None if isinstance(g, int) and g == G - 1 else (g + 1, 1 - q, s - S)

        def tiles(s):
            return slice(Q * s, Q * s + W_OF[s])

        def over(e, count, body, apart=0):
            for i in range(apart):
                body(i, 2 * i, 0)
                body(i, 2 * i + 1, 1)
            with e.Fori(apart, count // 2) as i:
                body(i, i * 2, 0)
                body(i, i * 2 + 1, 1)
            if count % 2:
                body(count // 2, count - 1, 0)

        def over_groups(e, body, apart=0):
            over(e, G, body, apart)

        def group_before(i, g, q):
            return None if isinstance(g, int) and g == 0 else (g - 1, 1 - q)

        def pair_through(j):
            return j + 3

        def block_range(e, g, which):
            both = e.value_load(rng_d[0:1, which, bass.ds(g, 1)], min_val=0, max_val=257 * (B - 1))
            return (e.snap(both & 255, min_val=0, max_val=B - 1),
                    e.snap(both >> 8, min_val=0, max_val=B - 1))

        N_LOADS = 21
        src_flat = src_i[:, :, :].rearrange("p g k -> p (g k)")
        dst_flat = dst_i[:, :, :].rearrange("p g k -> p (g k)")
        H_flat = H_all[:, :, :].rearrange("p b f -> p (b f)")

        def src_cols(g):
            return src_flat[:, bass.ds(g * K, K)]

        def dst_cols(g):
            return dst_flat[:, bass.ds(g * K, K)]

        def a_block(value):
            return nc.s_assert_within(value, 0, B - 1, skip_runtime_bounds_check_because=
                                      "the ranges hold block numbers of the nodes of edges")

        def make_high(e, v, g, q, data, parts, signal=True):
            i = nc.scalar.activation(parts, data, ACT.Copy)
            if signal:
                i.then_inc(v.high, 1)

        def make_rest1(e, v, g, data, parts):
            e.wait_ge(v.high, g + 3)
            nc.vector.tensor_tensor(data, data, parts[:, :, 0, 0:D], ALU.subtract).then_inc(v.rest1, 1)

        def make_mid(e, v, g, data, parts):
            e.wait_ge(v.rest1, g + 1)
            nc.scalar.activation(parts[:, :, 1, 0:D], data, ACT.Copy).then_inc(v.mid, 1)

        def make_rest2(e, v, g, data, parts):
            e.wait_ge(v.mid, g + 1)
            nc.vector.tensor_tensor(data, data, parts[:, :, 1, 0:D], ALU.subtract).then_inc(v.rest2, 1)

        def make_low(e, v, g, data, parts):
            e.wait_ge(v.rest2, g + 1)
            nc.scalar.activation(parts[:, :, 2, 0:D], data, ACT.Copy).then_inc(v.low, 1)

        def mark_and_add(e, regs, g, q, which, ids, table, width):
            seen, last_blk, last_row = regs
            lo, hi = block_range(e, g, which)
            with e.Fori(lo, hi + 1, 2) as blk:
                n = e.snap(seen)
                blk = a_block(blk)
                e.wait_ge(s_marks[S - 1], n + 1)
                nc.vector.tensor_scalar(local[:, q, :], ids[:, bass.ds(g * K, K)],
                                        block0[:, bass.ds(blk, 1)], None, ALU.subtract)\
                    .then_inc(s_local, 1)
                add_last(e, n, last_blk, last_row, table, width)
                e.wait_ge(s_local, n + 1)
                for s in range(S):
                    e.wait_ge(s_used[s], n + 1)
                    for k in range(Q * s, Q * s + W_OF[s]):
                        i = nc.vector.tensor_scalar(OH[:, k, :], iota_2[:, :], local[:, q, k:k + 1],
                                                    None, ALU.is_equal)
                    i.then_inc(s_marks[s], 1)
                e.reg_mov(last_row, q)
                e.reg_mov(last_blk, blk)
                e.reg_add(seen, seen, 1)

        def add_last(e, n, last_blk, last_row, table, width):
            first = e.snap(last_blk, min_val=0, max_val=B - 1) * width
            row = sums[:, bass.ds(e.snap(last_row, min_val=0, max_val=1), 1), 0:2 * width]
            e.wait_ge(s_used[S - 1], n + 1)
            e.wait_ge(s_added, n + 1)
            part = table[:, bass.ds(first, 2 * width)]
            nc.vector.tensor_tensor(part, part, row.rearrange("p a f -> p (a f)"), ALU.add)\
                .then_inc(s_added, 1)

        def sum_by_node(e, v, regs, g, q, which, parts, width):
            seen, free = regs
            lo, hi = block_range(e, g, which)
            e.reg_add(free, seen, 1)
            with e.Fori(lo, hi + 1, 2):
                n = e.snap(seen)
                e.wait_ge(s_added, e.snap(free))
                nc.tensor.matmul(sums[:, q, 0:2 * width], ones_b[0:1, :], zeros_b[:, 0:2 * width],
                                 start=True, stop=False)
                for s in range(S):
                    e.wait_ge(s_marks[s], n + 2)
                    for k in range(Q * s, Q * s + W_OF[s]):
                        for half in range(2):
                            for t in range(3):
                                w = width if t == 0 else D
                                mm = nc.tensor.matmul(sums[:, q, half * width:half * width + w],
                                                      OH[:, k, half * P:(half + 1) * P],
                                                      parts[:, k, t, 0:w], start=False, stop=False)
                    if s == S - 1:
                        mm = nc.tensor.matmul(sums[:, q, 0:2 * width], ones_b[0:1, :],
                                              zeros_b[:, 0:2 * width], start=False, stop=True)
                    mm.then_inc(s_used[s], 1)
                e.reg_add(seen, seen, 1)
                e.reg_add(free, seen, 2)
            nc.tensor.matmul(bank[5][0:1, 0:1] if v is not v2 else bank[0][0:1, 0:1], ones_b[0:1, 0:1],
                             zeros_b[:, 0:1], start=True, stop=True).then_inc(v.done, 1)

        def first_row(e, regs):
            e.reg_mov(regs[1], 0)
            e.reg_mov(regs[2], 1)

        def open_visits(e, regs):
            for counter in (s_local, *s_marks):
                e.sem_inc(counter, 1)
            e.reg_add(regs[0], regs[0], 1)
            first_row(e, regs)

        def open_sums(e, regs, width):
            for s in range(S - 1):
                e.sem_inc(s_used[s], 1)
            nc.tensor.matmul(sums[:, 1, 0:2 * width], ones_b[0:1, :], zeros_b[:, 0:2 * width],
                             start=True, stop=True).then_inc(s_used[S - 1], 1)
            if regs is not None:
                e.reg_add(regs[0], regs[0], 1)

        def in_bank(c):
            return bank[c][:, 0:min(8, K - 8 * c) * D].rearrange("p (k f) -> p k f", f=D)

        def row_of(v, n):
            return v.rearrange("(a n) -> a n", a=1) if n is None else \
                v.rearrange("(a n) -> a n", a=1).to_broadcast([n, v.shape[0]])

        @block.sync
        def _(e):
            e.dma_start(dst_g[0:G, :], dst.rearrange("(g e) -> g e", e=GE)).then_inc(s_dg, 16)
            e.wait_ge(s_wzero, 1)
            e.dma_start(X[:, 0:B - 1, :],
                        x[0:(B - 1) * P, :].rearrange("(b p) f -> p b f", p=P)).then_inc(s_xld, 16)
            e.dma_start(X[0:NL, B - 1, :], x[(B - 1) * P:N, :]).then_inc(s_xld, 16)
            for i_sb, i_dr in ((src_i, src), (dst_i, dst)):
                e.dma_start(i_sb[:, :, :], i_dr.rearrange("(g p k) -> p g k", p=P, k=K)).then_inc(s_ids, 16)

            def spread_ranges(n):
                e.wait_ge(s_rngd, n + 1)
                e.dma_start(range_dram[n:n + 1, 0:G].rearrange("a g -> g a"), rng_i[0:G, 0:1])\
                    .then_inc(s_rngst, 16)
                e.wait_ge(s_rngst, 16 * (n + 1))
                e.dma_start(rng_d[0:1, n, 0:G], range_dram[n:n + 1, 0:G]).then_inc(s_rngld[n], 16)
            spread_ranges(0)

            def load_pair(i, j, q):
                e.wait_ge(s_xT, pair_through(j - 2))
                slot = ea[:, q, 0:4, :].rearrange("p k f -> p (k f)").rearrange("p (b f) -> p b f", b=2)
                if isinstance(j, int) and j == NP - 1:
                    e.dma_start(slot[:, 0, :], x[(B - 2) * P:(B - 1) * P, :]).then_inc(s_xr[q], 16)
                    e.dma_start(slot[0:NL, 1, :], x[(B - 1) * P:N, :]).then_inc(s_xr[q], 16)
                else:
                    e.dma_start(slot, x[bass.ds(j * (2 * P), 2 * P), :]
                                .rearrange("(b p) f -> p b f", p=P)).then_inc(s_xr[q], 16)
            over(e, NP, load_pair)

            e.wait_ge(s_nc, pair_through(NP - 1))
            e.dma_start(node_rows.rearrange("(b p) f -> p b f", p=P), U[:, :, :]).then_inc(s_nst, 16)

            def load_features(i, g, q):
                first = e.snap(g * GE)
                e.wait_ge(s_tp, through(step(g - 2, S - 1)))
                e.dma_start(ea[:, q, :, :],
                            edge_attr[bass.ds(first, GE), :].rearrange("(p k) f -> p k f", k=K))\
                    .then_inc(s_ea[q], 16)
                e.wait_ge(s_msg, through(step(g - 2, S - 1)))
                e.sem_inc(s_turn["sync"], 1)
                e.dma_start(idx[:, q, :], src[bass.ds(first, GE)].rearrange("(p k) -> p k", k=K))\
                    .then_inc(s_idx[q], 16)
            over_groups(e, load_features)

            spread_ranges(1)

            e.wait_ge(s_g1, 1)
            def load_dst_row(i, g, q):
                first = e.snap(g * GE)
                e.wait_ge(s_pi, g + 1)
                e.dma_start(dst_row[:, q, :], dst[bass.ds(first, GE)]
                            .rearrange("(a e) -> a e", a=1).to_broadcast([P, GE])).then_inc(s_row[q], 16)
            over_groups(e, load_dst_row)

            for q in range(2):
                e.wait_ge(s_sc[q], 16 * K * ((G + 1 - q) // 2))
            def load_sorted(i, g, q):
                first = e.snap(g * GE)
                e.wait_ge(v4.done, g + 1)
                e.dma_start(rec[:, q, :, :],
                            sorted_rows[bass.ds(first, GE), :].rearrange("(p k) f -> p k f", k=K))\
                    .then_inc(s_m[q], 16)
            over_groups(e, load_sorted)
            e.wait_ge(s_g2, 1)
            e.dma_start(hop_rows.rearrange("(b p) f -> p b f", p=P), U[:, :, :]).then_inc(s_g2st, 16)

            def load_indices(i, g, q):
                first = e.snap(g * K)
                e.wait_ge(v6.high, g + 1)
                e.dma_start(idx[:, q, :], dst_flat[:, bass.ds(first, K)]).then_inc(s_ix6[q], 16)
            over_groups(e, load_indices)

            e.wait_ge(s_fin, 1)
            e.dma_start(out[0:(B - 1) * P, :].rearrange("(b p) f -> p b f", p=P), H[:, 0:B - 1, :])\
                .then_inc(s_out, 16)
            e.dma_start(out[(B - 1) * P:N, :], H[0:NL, B - 1, :]).then_inc(s_out, 16)
            e.wait_ge(s_out, 32)

        @block.gpsimd
        def _(e):
            e.memset(ident[:, :], 0.0).then_inc(s_fill, 1)
            e.memset(upper_f[:, :], 1.0).then_inc(s_fill, 1)
            e.memset(ones_b[:, :], 1.0).then_inc(s_fill, 1)
            e.memset(zeros_b[:, :], 0.0)
            e.memset(ones_f[:, :], 1.0)
            small = dict(channel_multiplier=0, allow_small_or_imprecise_dtypes=True)
            e.iota(iota_n[:, :], [[1, P]], base=0, **small)
            e.iota(iota_2[:, :], [[1, 2 * P]], base=0, **small)
            e.iota(block0[:, :], [[P, B + 1]], base=0, **small)
            lanes = dict(allow_small_or_imprecise_dtypes=True)
            e.iota(node_id[:, :], [[P, B]], base=0, channel_multiplier=1, **lanes)
            e.iota(thr[:, 0:1], [[0, 1]], base=0, channel_multiplier=GE, **lanes)
            e.iota(thr[:, 1:2], [[0, 1]], base=GE - 1, channel_multiplier=GE, **lanes)
            e.wait_ge(s_fill, 3)
            e.affine_select(out=ident[:, :], in_=ident[:, :], compare_op=ALU.not_equal, fill=1.0,
                            base=0, pattern=[[-1, P]], channel_multiplier=1)
            e.affine_select(out=upper[:, :], in_=ones_b[:, :], compare_op=ALU.is_gt, fill=0.0,
                            base=0, pattern=[[1, P]], channel_multiplier=-1)
            e.affine_select(out=upper_f[:, :], in_=upper_f[:, :], compare_op=ALU.is_gt, fill=0.0,
                            base=0, pattern=[[1, P]], channel_multiplier=-1).then_inc(s_const, 1)

            e.wait_ge(s_ids, 32)
            def gather_nodes(i, g, q):
                e.wait_ge(s_msg, through(step(g - 2, S - 1)))
                e.wait_ge(s_idx[q], (i + 1) * 16)
                e.wait_ge(s_nst, 16)
                e.sem_inc(s_turn["gpsimd"], 1)
                for k in range(K):
                    e.indirect_dma_start(
                        out=rows[:, q, k, :], out_offset=None, in_=node_rows,
                        in_offset=bass.IndirectOffsetOnAxis(ap=idx[:, q, k:k + 1], axis=0),
                    ).then_inc(s_rows[q][k // Q], 16)
            over_groups(e, gather_nodes)

            def scatter_rows(i, g, q):
                e.wait_ge(v4.low, g + 2)
                e.wait_ge(s_pi, g + 3)
                e.sem_inc(s_turn["gpsimd"], 1)
                for k in range(K):
                    e.indirect_dma_start(
                        out=sorted_rows,
                        out_offset=bass.IndirectOffsetOnAxis(ap=pos_i[:, q, k:k + 1], axis=0),
                        in_=rec[:, q, k, :], in_offset=None).then_inc(s_sc[q], 16)
            over_groups(e, scatter_rows)

            e.wait_ge(s_g2st, 16)
            def gather_hop(i, g, q):
                e.wait_ge(v6.low, g + 1)
                e.wait_ge(s_ix6[q], (i + 1) * 16)
                e.wait_ge(s_g2st, 16)
                e.sem_inc(s_turn["gpsimd"], 1)
                for k in range(K):
                    e.indirect_dma_start(
                        out=rows[:, q, k, :], out_offset=None, in_=hop_rows,
                        in_offset=bass.IndirectOffsetOnAxis(ap=idx[:, q, k:k + 1], axis=0),
                    ).then_inc(s_rows6[q], 16)
            over_groups(e, gather_hop)

        @block.scalar
        def _(e):
            e.wait_ge(s_wzero, 1)
            loads = [(w1n[0:D, 0, :], W1n), (w1n[D:P, 1, :], W1n), (w2n[:, :], W2n),
                     (b1n_c[:, :], b1n.rearrange("(n a) -> n a", a=1)), (b2n_r[:, :], row_of(b2n, None)),
                     (w2e[0:D, 0, :], W2e), (w2e[D:P, 1, :], W2e), (b2e_f[:, :], row_of(b2e, 3)),
                     (b1e_c[0:D, :], b1e.rearrange("(n a) -> n a", a=1)),
                     (b1e_c[D:P, :], b1e.rearrange("(n a) -> n a", a=1)),
                     (w_sb[:, 0, :], W), (w_sb[:, 1, :], W), (b_r[:, :], row_of(b, None)),
                     (gam[:, :], row_of(gamma, P)), (bet[:, :], row_of(beta, P)),
                     (scl[:, 0:1], row_of(dp_scale, P)), (scl[:, 1:2], row_of(res_w, P))]
            for t in range(Q):
                loads.append((w1e[DE * t:DE * (t + 1), t // 2, D * (t % 2):D * (t % 2) + D], W1e))
            assert len(loads) == N_LOADS
            for to, of in loads:
                e.dma_start(to, of).then_inc(s_load, 16)

            e.sem_inc(s_xTs, 2)
            e.sem_inc(s_nb, 2)
            e.wait_ge(s_load, 16 * N_LOADS)
            def node_copies(i, j, q):
                e.wait_ge(s_xT, pair_through(j))
                e.wait_ge(s_n1, pair_through(j - 2))
                nc.scalar.activation(eaT[:, q, :], bank[0][:, q * P:(q + 1) * P],
                                     ACT.Copy).then_inc(s_xTs, 1)
                e.wait_ge(s_n1, pair_through(j))
                e.wait_ge(s_nl, pair_through(j - 2))
                nc.scalar.activation(hb[:, q, :], bank[1 + q][:, 0:2 * P], ACT.Identity,
                                     bias=b1n_c[:, :]).then_inc(s_nb, 1)
            over(e, NP, node_copies)

            e.sem_inc(s_tc, BIAS)
            e.sem_inc(s_eb, BIAS)
            def copy_transpose(g, s):
                w = W_OF[s] * DE
                e.wait_ge(s_tp, through(step(g, s)))
                e.wait_ge(s_l1, through(before4(g, s)))
                nc.scalar.activation(eaT[0:w, s % 4, :], bank[0][0:w, 0:P], ACT.Copy).then_inc(s_tc, 1)

            def add_bias(g, s):
                parts, cols = (P, 2 * P) if W_OF[s] == Q else (D, P)
                e.wait_ge(s_l1, through(step(g, s)))
                e.wait_ge(s_lk, through(before4(g, s)))
                nc.scalar.activation(hb[0:parts, s % 4, 0:cols], hidden(s)[0:parts, 0:cols],
                                     ACT.Identity, bias=b1e_c[0:parts, :]).then_inc(s_eb, 1)

            copy_transpose(0, 0)
            copy_transpose(0, 1)
            add_bias(0, 0)
            copy_transpose(0, 2)
            add_bias(0, 1)
            def high_of_step(g, q, s):
                e.wait_ge(s_msg, through(step(g, s)))
                make_high(e, v2, g, q, msg[:, q, tiles(s), 0:D], parts_2[:, q, tiles(s), 0, 0:D],
                          signal=(s == S - 1))

            e.sem_inc(v2.high, 2)
            e.sem_inc(v2.low, 2)
            def edge_copies(i, g, q):
                for s in range(S):
                    if (t := ahead(g, q, s + 3)) is not None:
                        copy_transpose(t[0], t[2])
                    if (t := ahead(g, q, s + 2)) is not None:
                        add_bias(t[0], t[2])
                    if s == 1:
                        e.wait_ge(v2.done, g + 1)
                    if s > 0:
                        high_of_step(g, q, s - 1)
                    if s == 3 and (t := group_before(i, g, q)) is not None:
                        make_low(e, v2, t[0], msg[:, t[1], :, 0:D], parts_2[:, t[1]])
                high_of_step(g, q, S - 1)
                make_mid(e, v2, g, msg[:, q, :, 0:D], parts_2[:, q])
            over_groups(e, edge_copies, apart=1)
            make_low(e, v2, G - 1, msg[:, 0, :, 0:D], parts_2[:, 0])

            def deviation(n):
                e.wait_ge(s_var, n + 1)
                nc.scalar.activation(std[:, :], var[:, :], ACT.Sqrt).then_inc(s_dev, 1)
            for n in range(3):
                deviation(n)

            e.sem_inc(v4.low, 1)
            def rows_out(i, g, q):
                if not isinstance(i, int) or i > 0:
                    e.wait_ge(s_sc[q], i * (16 * K))
                nc.scalar.activation(rec[:, q, :, IDS:IDS + 1].bitcast(i32), src_cols(g).unsqueeze(2), ACT.Copy)
                nc.scalar.activation(rec[:, q, :, IDS + 1:R].bitcast(i32), dst_cols(g).unsqueeze(2), ACT.Copy)
                e.wait_ge(s_sel, g + 1)
                for c in range(4):
                    k, w = 8 * c, min(8, K - 8 * c)
                    last = nc.scalar.activation(rec_bf16[:, q, k:k + w, 0:D], in_bank(c), ACT.Copy)
                last.then_inc(v4.high, 1)
                e.wait_ge(v4.rest1, g + 2)
                nc.scalar.activation(rec_bf16[:, q, :, D:2 * D], rest4, ACT.Copy).then_inc(v4.mid, 1)
                e.wait_ge(v4.rest2, g + 1)
                nc.scalar.activation(rec_bf16[:, q, :, 2 * D:3 * D], rest4, ACT.Copy).then_inc(v4.low, 1)
            over_groups(e, rows_out, apart=1)

            def keep_ids(i, g, q):
                e.wait_ge(s_m[q], (i + 1) * 16)
                nc.scalar.activation(src_cols(g).unsqueeze(2), rec[:, q, :, IDS:IDS + 1].bitcast(i32), ACT.Copy)
                nc.scalar.activation(dst_cols(g).unsqueeze(2), rec[:, q, :, IDS + 1:R].bitcast(i32), ACT.Copy)\
                    .then_inc(s_srt, 1)
            over_groups(e, keep_ids)

            e.sem_inc(v6.high, 2)
            e.sem_inc(v6.low, 2)
            def split_hop(i, g, q):
                e.wait_ge(v6.done, g + 1)
                e.wait_ge(s_rows6[q], (i + 1) * (16 * K))
                make_high(e, v6, g, q, rows[:, q, :, :], parts_6[:, q, :, 0, 0:D])
                make_mid(e, v6, g, rows[:, q, :, :], parts_6[:, q])
                make_low(e, v6, g, rows[:, q, :, :], parts_6[:, q])
            over_groups(e, split_hop)

            e.wait_ge(s_wT, 1)
            for h in range(2):
                last = nc.scalar.activation(wT[h * D:(h + 1) * D, h, :], bank[3][h * D:(h + 1) * D, 0:D],
                                            ACT.Copy)
            last.then_inc(s_wTs, 1)
            e.sem_inc(s_hTs, 2)
            def h2_copies(i, j, q):
                e.wait_ge(s_hT, pair_through(j))
                e.wait_ge(s_lin, pair_through(j - 2))
                nc.scalar.activation(eaT[:, q, :], bank[0][:, q * P:(q + 1) * P],
                                     ACT.Copy).then_inc(s_hTs, 1)
            over(e, NP, h2_copies)
            deviation(3)

        @block.tensor
        def _(e):
            regs = [e.alloc_register(f"pe_{name}") for name in ("seen", "free")]
            seen4 = e.alloc_register("pe_seen4")
            for r in (regs[0], seen4):
                e.reg_mov(r, 0)
            for s_of, n in ((s_xT, 2), (s_n1, 2), (s_n2, 2), (s_tp, BIAS), (s_l1, BIAS), (s_l2, BIAS),
                            (s_hist, BIAS), (s_pa, BIAS), (v2.done, 2), (v4.done, 2), (v6.done, 2), (s_hT, 2), (s_lin, 2)):
                e.sem_inc(s_of, n)
            for s in range(S):
                e.sem_inc(s_u4[s], 1)
            e.wait_ge(s_const, 1)
            e.wait_ge(s_load, 16 * N_LOADS)

            def node_network(i, j, q):
                e.wait_ge(s_xr[q], (i + 1) * 16 if not (isinstance(j, int) and j == NP - 1) else (i + 2) * 16)
                e.wait_ge(s_xTs, pair_through(j - 2))
                nc.tensor.transpose(bank[0][:, q * P:(q + 1) * P],
                                    ea[:, q, 0:4, :].rearrange("p k f -> p (k f)"), ident[:, :])\
                    .then_inc(s_xT, 1)
                e.wait_ge(s_xTs, pair_through(j))
                e.wait_ge(s_nb, pair_through(j - 2))
                for h in range(2):
                    mm = nc.tensor.matmul(bank[1 + q][:, h * P:(h + 1) * P], w1n[:, h, :],
                                          eaT[:, q, :], start=True, stop=True)
                mm.then_inc(s_n1, 1)
                e.wait_ge(s_nl, pair_through(j))
                e.wait_ge(s_nc, pair_through(j - 2))
                for h in range(2):
                    o = bank[3 + q][:, h * D:(h + 1) * D]
                    nc.tensor.matmul(o, ones_f[:, :], b2n_r[:, :], start=True, stop=False)
                    mm = nc.tensor.matmul(o, hl[:, q, h * P:(h + 1) * P], w2n[:, :], start=False, stop=True)
                mm.then_inc(s_n2, 1)
            over(e, NP, node_network)

            e.wait_ge(s_rngld[0], 16)
            open_sums(e, None, D + 1)
            nc.tensor.matmul(bank[5][0:B, 0:1], ones_b[0:1, 0:B], zeros_b[:, 0:1], start=True, stop=False)
            def transpose(g, q, s):
                w = W_OF[s] * DE
                e.wait_ge(s_tc, through(step(g, s) - 1))
                nc.tensor.transpose(bank[0][0:w, 0:P],
                                    ea[:, q, tiles(s), :].rearrange("p k f -> p (k f)"), ident[:, :])\
                    .then_inc(s_tp, 1)

            def layer1(g, s):
                e.wait_ge(s_tc, through(step(g, s)))
                e.wait_ge(s_eb, through(before(g, s)))
                o = hidden(s)
                if W_OF[s] == Q:
                    for h in range(2):
                        mm = nc.tensor.matmul(o[:, h * P:(h + 1) * P], w1e[:, h, :], eaT[:, s % 4, :],
                                              start=True, stop=True)
                else:
                    mm = nc.tensor.matmul(o[0:D, 0:P], w1e[0:DE, 0, 0:D], eaT[0:DE, s % 4, :],
                                          start=True, stop=True)
                mm.then_inc(s_l1, 1)

            def layer2(g, s):
                w = W_OF[s]
                e.wait_ge(s_lk, through(step(g, s)))
                e.wait_ge(s_msg, through(before(g, s)))
                o = edge_out(s)
                nc.tensor.matmul(o[:, 0:w * D], ones_b[0:3, :],
                                 b2e_3[:, :].unsqueeze(1).to_broadcast([3, w, D]), start=True, stop=False)
                if w == Q:
                    for h in range(2):
                        mm = nc.tensor.matmul(o[:, h * P:(h + 1) * P], hl[:, s % 4, h * P:(h + 1) * P],
                                              w2e[:, :, :].rearrange("p t f -> p (t f)"),
                                              start=False, stop=(h == 1))
                else:
                    mm = nc.tensor.matmul(o[:, 0:D], hl[0:D, s % 4, 0:P], w2e[0:D, 0, :],
                                          start=False, stop=True)
                mm.then_inc(s_l2, 1)

            e.wait_ge(s_b3, 1)
            e.wait_ge(s_ea[0], 16)
            transpose(0, 0, 0)
            transpose(0, 0, 1)
            layer1(0, 0)
            transpose(0, 0, 2)
            layer1(0, 1)
            def edge_network(i, g, q):
                for s in range(S):
                    if (t := ahead(g, q, s + 3)) is not None:
                        if t[2] == 0:
                            e.wait_ge(s_ea[1 - q], (i + 1 + q) * 16)
                        transpose(*t)
                    if (t := ahead(g, q, s + 2)) is not None:
                        layer1(t[0], t[2])
                    layer2(g, s)
                    e.wait_ge(s_ob, through(step(g, s)))
                    for k in range(W_OF[s]):
                        mm = nc.tensor.matmul(bank[5][0:B, 0:1], ob[:, s % 2, k, :], ones_b[:, 0:1],
                                              start=False, stop=False)
                    mm.then_inc(s_hist, 1)
                if (t := group_before(i, g, q)) is not None:
                    e.wait_ge(v2.low, t[0] + 3)
                    sum_by_node(e, v2, regs, *t, 0, parts_2[:, t[1]], D + 1)
            over_groups(e, edge_network, apart=1)
            e.wait_ge(v2.low, G - 1 + 3)
            sum_by_node(e, v2, regs, G - 1, 0, 0, parts_2[:, 0], D + 1)
            nc.tensor.matmul(bank[5][0:B, 0:1], ones_b[0:1, 0:B], zeros_b[:, 0:1], start=False, stop=True)\
                .then_inc(s_total, 1)

            e.wait_ge(s_cT, 1)
            nc.tensor.matmul(bank[4][:, 0:B], counts_T[0:B, :], upper_f[0:B, 0:B], start=True, stop=True)\
                .then_inc(s_bases, 1)

            e.wait_ge(s_g1, 1)
            def select_rows(i, g, q):
                e.wait_ge(v4.rest1, g + 1)
                for c in range(4):
                    nc.tensor.matmul(bank[c][:, :], ones_b[0:1, :], zeros_b[:, :], start=True, stop=False)
                lo, hi = block_range(e, g, 0)
                with e.Fori(lo, hi + 1) as blk:
                    n = e.snap(seen4)
                    blk = a_block(blk)
                    for s in range(S):
                        e.wait_ge(s_m4[s], n + 1)
                        for k in range(Q * s, Q * s + W_OF[s]):
                            for part in g1_parts:
                                mm = nc.tensor.matmul(bank[k // 8][:, (k % 8) * D:(k % 8 + 1) * D], OH4[:, k, :],
                                                      part[:, bass.ds(blk, 1), :].rearrange("p a f -> p (a f)"),
                                                      start=False, stop=False)
                        mm.then_inc(s_u4[s], 1)
                    e.reg_add(seen4, seen4, 1)
                for c in range(4):
                    mm = nc.tensor.matmul(bank[c][:, :], ones_b[0:1, :], zeros_b[:, :], start=False, stop=True)
                mm.then_inc(s_sel, 1)

                for s in range(S):
                    w = W_OF[s]
                    rank = bank[4 + s % 2][:, 0:(Q + 1) * B].rearrange("p (k b) -> p k b", b=B)
                    e.wait_ge(s_ob4, through(step(g, s)))
                    e.wait_ge(s_pl, through(before(g, s)))
                    nc.tensor.matmul(rank[:, 0:w + 1, :], ones_b[0:1, :], zeros_b[:, 0:(w + 1) * B],
                                     start=True, stop=False)
                    for k in range(w):
                        nc.tensor.matmul(rank[:, k, :], upper[:, :], ob[:, s % 3, k, :],
                                         start=False, stop=False)
                        n = w - k
                        mm = nc.tensor.matmul(rank[:, k + 1:w + 1, :], ones_b[:, :],
                                              ob[:, s % 3, k:k + 1, :].to_broadcast([P, n, B]),
                                              start=False, stop=(k == w - 1))
                    mm.then_inc(s_pa, 1)
            over_groups(e, select_rows)

            e.wait_ge(s_rngld[1], 16)
            open_sums(e, regs, D)
            def sum_sorted(i, g, q):
                e.wait_ge(s_m[q], (i + 1) * 16)
                sum_by_node(e, v4, regs, g, q, 1,
                            rec_bf16[:, q, :, 0:3 * D].rearrange("p k (t f) -> p k t f", t=3), D)
            over_groups(e, sum_sorted)
            e.wait_ge(s_g2, 1)
            open_sums(e, regs, D)
            def sum_hop(i, g, q):
                e.wait_ge(v6.low, g + 3)
                sum_by_node(e, v6, regs, g, q, 1, parts_6[:, q], D)
            over_groups(e, sum_hop)

            nc.tensor.transpose(bank[3][:, 0:D], w_sb[:, :, :].rearrange("p a f -> p (a f)"),
                                ident[0:D, 0:D]).then_inc(s_wT, 1)
            e.wait_ge(s_wTs, 1)
            def last_product(i, j, q):
                e.wait_ge(s_h2, pair_through(j))
                e.wait_ge(s_hTs, pair_through(j - 2))
                nc.tensor.transpose(bank[0][:, q * P:(q + 1) * P],
                                    hb[:, q, 0:P], ident[:, :]).then_inc(s_hT, 1)
                e.wait_ge(s_hTs, pair_through(j))
                e.wait_ge(s_res, pair_through(j - 2))
                for h in range(2):
                    o = bank[1 + q][:, h * D:(h + 1) * D]
                    nc.tensor.matmul(o, ones_f[:, :], b_r[:, :], start=True, stop=False)
                    mm = nc.tensor.matmul(o, eaT[:, q, :], wT[:, h, :],
                                          start=False, stop=True)
                mm.then_inc(s_lin, 1)
            over(e, NP, last_product)

        @block.vector
        def _(e):
            done = [0]

            def link(ins):
                done[0] += 1
                ins.then_inc(s_dv, 1)
                e.wait_ge(s_dv, done[0])

            regs = [e.alloc_register(f"dve_{name}") for name in ("seen", "blk", "row")]
            seen4 = e.alloc_register("dve_seen4")
            e.reg_mov(regs[0], 0)
            e.reg_mov(seen4, 0)
            first_row(e, regs)

            def pack_ranges(low_high):
                link(nc.vector.scalar_tensor_tensor(
                    out=rng_f[0:G, 0:1], in0=low_high[0:G, 1:2], scalar=256.0, in1=low_high[0:G, 0:1],
                    op0=ALU.mult, op1=ALU.add))
                nc.vector.tensor_copy(rng_i[0:G, 0:1], rng_f[0:G, 0:1]).then_inc(s_rngd, 1)

            for s_of, n in ((s_nl, 2), (s_nc, 2), (s_lk, BIAS), (s_msg, BIAS), (s_ob, BIAS), (s_ob4, BIAS),
                            (s_pl, BIAS), (s_run, BIAS), (s_pm, BIAS), (s_pr, BIAS), (s_pi, 2),
                            (s_h2, 2), (s_res, 2)):
                e.sem_inc(s_of, n)
            for counter in (s_added, *s_marks, v4.rest1):
                e.sem_inc(counter, 1)
            nc.vector.memset(w1e[:, :, :], 0.0)
            nc.vector.memset(w2e[:, :, :], 0.0)
            nc.vector.memset(w1n[:, :, :], 0.0)
            nc.vector.memset(wT[:, :, :], 0.0)
            nc.vector.memset(X[:, B - 1, :], 0.0)
            nc.vector.memset(ea[:, :, :, :], 0.0).then_inc(s_wzero, 1)

            e.wait_ge(s_dg, 16)
            link(nc.vector.tensor_reduce(rng_f[0:G, 0:1], dst_g[0:G, :], AX.X, ALU.min))
            link(nc.vector.tensor_reduce(rng_f[0:G, 1:2], dst_g[0:G, :], AX.X, ALU.max))
            link(nc.vector.tensor_copy(rng_i[0:G, :], rng_f[0:G, :]))
            link(nc.vector.tensor_scalar(rng_i[0:G, :], rng_i[0:G, :], 7, None, ALU.arith_shift_right))
            pack_ranges(rng_i)
            nc.vector.memset(parts_2[:, :, :, 0, D:PW], 1.0)
            link(nc.vector.memset(tab[:, :], 0.0))

            def node_values(i, j, q):
                e.wait_ge(s_nb, pair_through(j))
                e.wait_ge(s_n2, pair_through(j - 2))
                nc.vector.scalar_tensor_tensor(out=hl[:, q, :], in0=hb[:, q, :], scalar=SLOPE,
                                               in1=hb[:, q, :], op0=ALU.mult, op1=ALU.max).then_inc(s_nl, 1)
                e.wait_ge(s_n2, pair_through(j))
                nc.vector.tensor_copy(U[:, bass.ds(j * 2, 2), :],
                                      bank[3 + q][:, 0:2 * D].rearrange("p (b f) -> p b f", f=D))\
                    .then_inc(s_nc, 1)
            over(e, NP, node_values)

            e.wait_ge(s_load, 16 * N_LOADS)
            e.wait_ge(s_const, 1)
            for part in range(3):
                link(nc.vector.tensor_copy(b2e_p[:, part, :], b2e_f[:, :]))
                link(nc.vector.tensor_tensor(b2e_f[:, :], b2e_f[:, :], b2e_p[:, part, :], ALU.subtract))
            link(nc.vector.tensor_scalar(b2e_3[:, :], b2e_p[:, 0, :], ident[0:3, 0:1], None, ALU.mult))
            for part in range(1, 3):
                link(nc.vector.scalar_tensor_tensor(
                    out=b2e_3[:, :], in0=b2e_p[:, part, :], scalar=ident[0:3, part:part + 1],
                    in1=b2e_3[:, :], op0=ALU.mult, op1=ALU.add))
            e.sem_inc(s_b3, 1)
            e.wait_ge(s_ids, 32)
            e.wait_ge(s_rngld[0], 16)

            def mark_buckets(s, q, signal, depth=2):
                w = W_OF[s]
                nc.vector.tensor_tensor(ob[:, s % depth, 0:w, :],
                                        bucket[:, q, tiles(s)].unsqueeze(2).to_broadcast([P, w, B]),
                                        iota_n[:, 0:B].unsqueeze(1).to_broadcast([P, w, B]),
                                        ALU.is_equal).then_inc(signal, 1)

            def leaky(g, s):
                parts, cols = (P, 2 * P) if W_OF[s] == Q else (D, P)
                e.wait_ge(s_eb, through(step(g, s)))
                e.wait_ge(s_l2, through(before4(g, s)))
                nc.vector.scalar_tensor_tensor(
                    out=hl[0:parts, s % 4, 0:cols], in0=hb[0:parts, s % 4, 0:cols], scalar=SLOPE,
                    in1=hb[0:parts, s % 4, 0:cols], op0=ALU.mult, op1=ALU.max).then_inc(s_lk, 1)

            leaky(0, 0)
            def messages(i, g, q):
                def message(s):
                    w = W_OF[s]
                    e.wait_ge(s_l2, through(step(g, s)))
                    e.wait_ge(s_rows[q][s], (i + 1) * (16 * w))
                    nc.vector.tensor_tensor(msg[:, q, tiles(s), 0:D],
                                            edge_out(s)[:, 0:w * D].rearrange("p (k f) -> p k f", f=D),
                                            rows[:, q, tiles(s), :], ALU.mult).then_inc(s_msg, 1)

                nc.vector.tensor_scalar(bucket[:, q, :], src_cols(g), 7, None,
                                        ALU.arith_shift_right).then_inc(s_bk, 1)
                e.wait_ge(s_bk, g + 1)
                e.wait_ge(v2.low, g + 1)
                for s in range(S):
                    if (t := ahead(g, q, s + 1)) is not None:
                        leaky(t[0], t[2])
                    e.wait_ge(s_hist, through(before(g, s)))
                    mark_buckets(s, q, s_ob)
                    if s > 0:
                        message(s - 1)
                message(S - 1)
                make_rest1(e, v2, g, msg[:, q, :, 0:D], parts_2[:, q])
                if (t := group_before(i, g, q)) is not None:
                    mark_and_add(e, regs, *t, 0, dst_flat, tab, D + 1)
                make_rest2(e, v2, g, msg[:, q, :, 0:D], parts_2[:, q])
            over_groups(e, messages, apart=1)
            mark_and_add(e, regs, G - 1, 0, 0, dst_flat, tab, D + 1)

            add_last(e, e.snap(regs[0]), regs[1], regs[2], tab, D + 1)
            e.wait_ge(s_added, e.snap(regs[0]) + 2)
            wide = [P, B, D]

            def spread(t):
                return t.unsqueeze(2).to_broadcast(wide)

            def norm(t, to, squares, n):
                link(nc.vector.tensor_reduce(mean[:, :], t, AX.X, ALU.add))
                link(nc.vector.tensor_scalar(mean[:, :], mean[:, :], 1.0 / D, None, ALU.mult))
                link(nc.vector.tensor_tensor(t, t, spread(mean[:, :]), ALU.subtract))
                link(nc.vector.tensor_tensor(squares, t, t, ALU.mult))
                link(nc.vector.tensor_reduce(var[:, :], squares, AX.X, ALU.add))
                nc.vector.tensor_scalar(var[:, :], var[:, :], 1.0 / D, EPS, ALU.mult, ALU.add)\
                    .then_inc(s_var, 1)
                e.wait_ge(s_dev, n + 1)
                link(nc.vector.reciprocal(std[:, :], std[:, :]))
                link(nc.vector.tensor_tensor(to, t, spread(std[:, :]), ALU.mult))

            e.wait_ge(s_load, 16 * N_LOADS)
            e.wait_ge(s_xld, 32)
            e.wait_ge(s_nst, 16)
            nc.vector.tensor_scalar(var[:, :], agg0[:, :, D], 1.0, None, ALU.add).then_inc(s_var, 1)
            link(nc.vector.tensor_tensor(scale[:, :], scl[:, 0:1], scl[:, 1:2], ALU.mult))
            link(nc.vector.scalar_tensor_tensor(out=U[:, :, :], in0=agg0[:, :, 0:D], scalar=scale[:, 0:1],
                                                in1=X[:, :, :], op0=ALU.mult, op1=ALU.add))
            e.wait_ge(s_dev, 1)
            link(nc.vector.reciprocal(dinv[:, :], std[:, :]))
            norm(U[:, :, :], U[:, :, :], H[:, :, :], 1)
            link(nc.vector.tensor_tensor(U[:, :, :], U[:, :, :], gam[:, :].unsqueeze(1).to_broadcast(wide), ALU.mult))
            link(nc.vector.tensor_tensor(U[:, :, :], U[:, :, :], bet[:, :].unsqueeze(1).to_broadcast(wide), ALU.add))
            link(nc.vector.tensor_tensor(U[:, :, :], U[:, :, :], X[:, :, :], ALU.add))
            norm(U[:, :, :], X[:, :, :], H[:, :, :], 2)
            link(nc.vector.tensor_tensor(U[:, :, :], X[:, :, :], spread(dinv[:, :]), ALU.mult))
            rest = tab[:, 0:B * D].rearrange("p (b f) -> p b f", f=D)
            link(nc.vector.tensor_copy(g1_parts[0], U[:, :, :]))
            link(nc.vector.tensor_tensor(rest, U[:, :, :], g1_parts[0], ALU.subtract))
            link(nc.vector.tensor_copy(g1_parts[1], rest))
            link(nc.vector.tensor_tensor(rest, rest, g1_parts[1], ALU.subtract))
            link(nc.vector.tensor_copy(g1_parts[2], rest))
            e.wait_ge(s_total, 1)
            nc.vector.tensor_copy(counts_T[0:B, :], bank[5][0:B, 0:1].to_broadcast([B, P])).then_inc(s_cT, 1)
            e.wait_ge(s_bases, 1)
            link(nc.vector.tensor_copy(place[:, 0, :], bank[4][:, 0:B]))
            for a in range(2):
                link(nc.vector.tensor_scalar(cmp_w[0:G, a, 0:B - 1], place[0:G, 0, 1:B], thr[0:G, a:a + 1],
                                             None, ALU.is_le))
            link(nc.vector.tensor_reduce(rng_f[0:G, :], cmp_w[0:G, :, 0:B - 1], AX.X, ALU.add))
            pack_ranges(rng_f)
            e.sem_inc(s_g1, 1)

            def marks_and_places(i, g, q):
                e.wait_ge(s_row[q], (i + 1) * 16)
                by_tile = dst_row[:, q, :].rearrange("p (e k) -> p k e", k=K)
                lo, hi = block_range(e, g, 0)
                with e.Fori(lo, hi + 1) as blk:
                    n = e.snap(seen4)
                    blk = a_block(blk)
                    for s in range(S):
                        e.wait_ge(s_u4[s], n + 1)
                        nc.vector.tensor_scalar(OH4[:, tiles(s), :], by_tile[:, tiles(s), :],
                                                node_id[:, bass.ds(blk, 1)], None,
                                                ALU.is_equal).then_inc(s_m4[s], 1)
                    e.reg_add(seen4, seen4, 1)

                nc.vector.tensor_scalar(bucket[:, q, :], src_cols(g), 7, None,
                                        ALU.arith_shift_right).then_inc(s_bk4, 1)
                e.wait_ge(s_bk4, g + 1)
                e.wait_ge(s_pr, through(step(g, 0) - 1))
                mark_buckets(0, q, s_ob4, 3)

                def add_places(s):
                    w = W_OF[s]
                    rank = bank[4 + s % 2][:, 0:(Q + 1) * B].rearrange("p (k b) -> p k b", b=B)
                    now, after = place[:, (q + s) % 2, :], place[:, (q + s + 1) % 2, :]
                    e.wait_ge(s_pa, through(step(g, s)))
                    e.wait_ge(s_run, through(step(g, s) - 1))
                    e.wait_ge(s_pl, through(step(g, s) - 1))
                    nc.vector.tensor_tensor(after, now, rank[:, w, :], ALU.add).then_inc(s_run, 1)
                    e.wait_ge(s_pr, through(step(g, s) - 3))
                    nc.vector.tensor_tensor(rank_w[:, s % 3, 0:w, :], rank[:, 0:w, :],
                                            now.unsqueeze(1).to_broadcast([P, w, B]),
                                            ALU.add).then_inc(s_pl, 1)

                def pick_place(s):
                    r = rank_w[:, s % 3, 0:W_OF[s], :]
                    e.wait_ge(s_pl, through(step(g, s)))
                    nc.vector.tensor_tensor(r, r, ob[:, s % 3, 0:W_OF[s], :], ALU.mult).then_inc(s_pm, 1)

                def sum_place(s):
                    e.wait_ge(s_pm, through(step(g, s)))
                    nc.vector.tensor_reduce(pos_f[:, q, tiles(s)], rank_w[:, s % 3, 0:W_OF[s], :], AX.X,
                                            ALU.add).then_inc(s_pr, 1)

                for s in range(S + 2):
                    if s < S:
                        add_places(s)
                    if s + 1 < S:
                        if s + 1 >= 3:
                            e.wait_ge(s_pm, through(step(g, s + 1) - 3))
                        mark_buckets(s + 1, q, s_ob4, 3)
                    if 1 <= s <= S:
                        pick_place(s - 1)
                    if s >= 2:
                        sum_place(s - 2)
                    if s == 3:
                        e.wait_ge(v4.high, g + 1)
                        e.wait_ge(v4.low, g + 1)
                        for c in range(4):
                            k, w = 8 * c, min(8, K - 8 * c)
                            last = nc.vector.tensor_tensor(rest4[:, k:k + w, :], in_bank(c),
                                                           rec_bf16[:, q, k:k + w, 0:D], ALU.subtract)
                        last.then_inc(v4.rest1, 1)
                    if s == 6:
                        e.wait_ge(v4.mid, g + 1)
                        nc.vector.tensor_tensor(rest4, rest4, rec_bf16[:, q, :, D:2 * D],
                                                ALU.subtract).then_inc(v4.rest2, 1)
                e.wait_ge(s_pr, through(step(g, S - 1)))
                nc.vector.tensor_copy(pos_i[:, q, :], pos_f[:, q, :]).then_inc(s_pi, 1)
            over_groups(e, marks_and_places)

            e.wait_ge(s_sel, G)
            nc.vector.memset(H_all[:, :, :], 0.0).then_inc(s_zero, 1)
            e.wait_ge(s_zero, 1)
            open_visits(e, regs)
            e.wait_ge(s_rngld[1], 16)
            def mark_sorted(i, g, q):
                e.wait_ge(s_srt, g + 1)
                mark_and_add(e, regs, g, q, 1, src_flat, H_flat, D)
            over_groups(e, mark_sorted)
            add_last(e, e.snap(regs[0]), regs[1], regs[2], H_flat, D)
            e.wait_ge(s_added, e.snap(regs[0]) + 2)
            link(nc.vector.tensor_tensor(H[:, :, :], H[:, :, :], U[:, :, :], ALU.add))
            link(nc.vector.tensor_tensor(H[:, :, :], H[:, :, :], spread(dinv[:, :]), ALU.mult))
            link(nc.vector.tensor_tensor(U[:, :, :], H[:, :, :], spread(dinv[:, :]), ALU.mult))
            nc.vector.memset(H_all[:, :, :], 0.0).then_inc(s_g2, 1)
            e.wait_ge(s_g2, 1)
            open_visits(e, regs)

            def mark_hop(i, g, q):
                make_rest1(e, v6, g, rows[:, q, :, :], parts_6[:, q])
                if (t := group_before(i, g, q)) is not None:
                    mark_and_add(e, regs, *t, 1, src_flat, H_flat, D)
                make_rest2(e, v6, g, rows[:, q, :, :], parts_6[:, q])
            over_groups(e, mark_hop, apart=1)
            mark_and_add(e, regs, G - 1, 0, 1, src_flat, H_flat, D)
            add_last(e, e.snap(regs[0]), regs[1], regs[2], H_flat, D)
            e.wait_ge(s_added, e.snap(regs[0]) + 2)
            e.sem_inc(s_turn["vector"], 1)

            def h2_and_residual(i, j, q):
                pair = bass.ds(j * 2, 2)
                h2 = hb[:, q, 0:P].rearrange("p (b f) -> p b f", f=D)
                e.wait_ge(s_hT, pair_through(j - 2))
                nc.vector.tensor_tensor(h2, H[:, pair, :], U[:, pair, :], ALU.add).then_inc(s_ha, 1)
                e.wait_ge(s_ha, j + 1)
                nc.vector.tensor_tensor(h2, h2, dinv[:, pair].unsqueeze(2).to_broadcast([P, 2, D]),
                                        ALU.mult).then_inc(s_h2, 1)
                e.wait_ge(s_lin, pair_through(j))
                nc.vector.tensor_tensor(H[:, pair, :], X[:, pair, :],
                                        bank[1 + q][:, 0:P].rearrange("p (b f) -> p b f", f=D),
                                        ALU.add).then_inc(s_res, 1)
            over(e, NP, h2_and_residual)
            e.wait_ge(s_res, pair_through(NP - 1))
            norm(H[:, :, :], H[:, :, :], U[:, :, :], 3)
            e.sem_inc(s_fin, 1)


_INS = ['x', 'src', 'dst', 'edge_attr_32', 'L0_gnn_W1n', 'L0_gnn_b1n', 'L0_gnn_W2n', 'L0_gnn_b2n',
        'L0_gnn_W1e', 'L0_gnn_b1e', 'L0_gnn_W2e', 'L0_gnn_b2e', 'L0_gnn_res_w', 'L0_gnn_dp_scale',
        'L0_gnn_gamma', 'L0_gnn_beta', 'L1_gnn_W', 'L1_gnn_b']


def kernel(**inputs):
    import numpy as np
    import concourse.bacc as bacc
    from concourse.bass_utils import run_bass_kernel_spmd

    nc = bacc.Bacc("TRN2", target_bir_lowering=False, num_devices=1)
    arrays, args = {}, []
    for name in _INS:
        a = np.ascontiguousarray(inputs[name])
        arrays[f"in_{name}"] = a
        args.append(nc.dram_tensor(f"in_{name}", a.shape, mybir.dt.from_np(a.dtype), kind="ExternalInput").ap())
    out = nc.dram_tensor("out", inputs["x"].shape, mybir.dt.float32, kind="ExternalOutput").ap()
    gnn_two_layers(nc, *args, out)
    r = run_bass_kernel_spmd(nc, [arrays], core_ids=[0])
    return r.results[0]["out"]
```
